# Optimizing a Trainium2 kernel written in Bass

```python
import numpy as np
import jax
import jax.numpy as jnp

def _softmax(x, axis=-1):
    return jax.nn.softmax(x, axis=axis)

def _gelu(x):
    return jax.nn.gelu(x, approximate=True)

def _silu(x):
    return jax.nn.silu(x)

def _sigmoid(x):
    return jax.nn.sigmoid(x)

def _layernorm(x, axis=-1, eps=1e-05):
    m = jnp.mean(x, axis=axis, keepdims=True)
    v = jnp.var(x, axis=axis, keepdims=True)
    return (x - m) / jnp.sqrt(v + eps)

def _scatter_add(tgt, idx, src, axis=0):
    return tgt.at[idx].add(src)

def _segment_sum(src, seg, n):
    return jax.ops.segment_sum(src, seg, n)
kernel_name = 'mk_decoder_preln_d1_seqx_r2_f2cef7'

def setup_inputs(seed: int=0):
    np.random.seed(seed)
    _w = jnp.asarray

    def _rec_inputs():
        import jax
        import jax.numpy as jnp
        _rk = jax.random.key(seed)
        x = -0.0002928 + 1 * jax.random.normal(jax.random.fold_in(_rk, 1), (8, 224, 512), jnp.float32)
        _lenS = 224 - jax.random.randint(jax.random.fold_in(_rk, 7), (8,), 0, max(1, 224 // 4) + 1, jnp.int32)
        _lenS2 = 750 - jax.random.randint(jax.random.fold_in(_rk, 8), (8,), 0, max(1, 750 // 4) + 1, jnp.int32)
        _ctx_1024P = jax.random.normal(jax.random.fold_in(_rk, 11), (8, 16, 512), jnp.float32)
        _ctx_1024c = jax.random.dirichlet(jax.random.fold_in(_rk, 511), 0.3 * jnp.ones((16,), jnp.float32), (8, 750))
        _ctx_1024t = jnp.einsum('bsk,bkd->bsd', _ctx_1024c, _ctx_1024P)
        _ctx_1024t = _ctx_1024t * jax.lax.rsqrt(jnp.mean(jnp.square(_ctx_1024t)) + 1e-12) * 0.953939
        ctx_1024 = -1.39393e-06 + 0.999914 * (_ctx_1024t + 0.3 * jax.random.normal(jax.random.fold_in(_rk, 611), (8, 750, 512), jnp.float32))
        _validS = jnp.arange(224)[None, :] < _lenS[:, None]
        _validS2 = jnp.arange(750)[None, :] < _lenS2[:, None]
        _causal = jnp.tril(jnp.ones((224, 224), dtype=bool))
        mask_1x1xSxS2_fk0 = jnp.where(jnp.broadcast_to(_validS2[0:1, None, None, :], (1, 1, 224, 750)), 0.0, 1.0).astype(jnp.float32)
        return (x, ctx_1024, mask_1x1xSxS2_fk0)
    x, ctx_1024, mask_1x1xSxS2_fk0 = _rec_inputs()

    def _L0_attn_setup():
        import math
        import jax, jax.numpy as jnp
        import numpy as np
        B, T, C = (2, 1024, 512)
        H, N1, N2, N3 = (16, 6, 4, 6)
        HD = C // H

        def _rotary(T_, hd, dtype):
            inv_freq = 1.0 / 10000.0 ** (jnp.arange(0, hd, 2, dtype=jnp.float32) / hd)
            freqs = jnp.outer(jnp.arange(T_, dtype=jnp.float32), inv_freq)
            return (jnp.cos(freqs)[None, :, None, :].astype(dtype), jnp.sin(freqs)[None, :, None, :].astype(dtype))

        def _apply_rot(x, cos, sin):
            x1, x2 = (x[..., :x.shape[-1] // 2], x[..., x.shape[-1] // 2:])
            return jnp.concatenate([x1 * cos + x2 * sin, -x1 * sin + x2 * cos], axis=-1).astype(x.dtype)

        def _causal_bias(L, S, dtype):
            mask = jnp.triu(jnp.ones((L, S), bool), k=1)
            return jnp.where(mask, jnp.asarray(-jnp.inf, dtype), jnp.asarray(0.0, dtype))

        def _sdpa(q, k, v, scale):
            scores = jnp.einsum('bhtd,bhsd->bhts', q, k) * scale + _causal_bias(q.shape[-2], k.shape[-2], q.dtype)
            return jnp.einsum('bhts,bhsd->bhtd', jax.nn.softmax(scores, axis=-1), v)

        def _hyp_attn(q, k, v, curv):
            eps = 1e-06
            tq = jnp.sqrt(1.0 / curv + jnp.sum(q * q, axis=-1, keepdims=True))
            tk = jnp.sqrt(1.0 / curv + jnp.sum(k * k, axis=-1, keepdims=True))
            inner = jnp.einsum('bhtd,bhsd->bhts', q, k) - tq * jnp.swapaxes(tk, -1, -2)
            arg = jnp.maximum(-curv * inner, 1.0 + 1e-07)
            dis = jnp.sqrt(1.0 / curv) * jnp.arccosh(arg)
            scores = 1.0 / (eps + dis) + _causal_bias(q.shape[-2], k.shape[-2], q.dtype)
            return jnp.einsum('bhts,bhsd->bhtd', jax.nn.softmax(scores, axis=-1), v)
        key = jax.random.key(seed)
        k1, k2, k3 = jax.random.split(key, 3)
        return {'x': jax.random.normal(k1, (B, T, C), jnp.float32), 'qkv_w': jax.random.normal(k2, (3 * C, C), jnp.float32) * C ** (-0.5), 'proj_w': jax.random.normal(k3, (C, C), jnp.float32) * C ** (-0.5), 'proj_b': jnp.zeros((C,), jnp.float32), 'curvature': jnp.ones((1, N2, 1, 1), jnp.float32)}
    _L0_attn_all = _L0_attn_setup()
    _L0_attn_in = {k: v for k, v in _L0_attn_all.items() if k in ('qkv_w', 'proj_w', 'proj_b', 'curvature')}
    del _L0_attn_all

    def _L0_xattn_setup():
        import jax, jax.numpy as jnp
        import numpy as np
        B, T, E, H = (2, 1024, 512, 16)
        key = jax.random.key(seed)
        ks = jax.random.split(key, 8)
        std = 1.0 / np.sqrt(E)
        x = jax.random.normal(ks[0], (B, T, E), dtype=jnp.float32)
        y = jax.random.normal(ks[1], (B, T, E), dtype=jnp.float32)
        mask = jnp.tril(jnp.ones((T, T), dtype=jnp.float32))[None, None]
        Wq = jax.random.normal(ks[2], (E, E), dtype=jnp.float32) * std
        Wk = jax.random.normal(ks[3], (E, E), dtype=jnp.float32) * std
        Wv = jax.random.normal(ks[4], (E, E), dtype=jnp.float32) * std
        Wo = jax.random.normal(ks[5], (E, E), dtype=jnp.float32) * std
        bq = jnp.zeros((E,), jnp.float32)
        bk = jnp.zeros((E,), jnp.float32)
        bv = jnp.zeros((E,), jnp.float32)
        bo = jnp.zeros((E,), jnp.float32)
        return {'x': x, 'y': y, 'mask': mask, 'Wq': Wq, 'bq': bq, 'Wk': Wk, 'bk': bk, 'Wv': Wv, 'bv': bv, 'Wo': Wo, 'bo': bo, 'num_heads': H}
    _L0_xattn_all = _L0_xattn_setup()
    _L0_xattn_in = {k: v for k, v in _L0_xattn_all.items() if k in ('Wq', 'bq', 'Wk', 'bk', 'Wv', 'bv', 'Wo', 'bo')}
    del _L0_xattn_all

    def _L0_ffn_setup():
        import jax, jax.numpy as jnp
        import numpy as np
        H = 8
        KD = 128
        TOPK = 8
        NUM_KEYS = 128
        N_EXPERTS = NUM_KEYS * NUM_KEYS
        N_DIM = 512
        BN_EPS = 1e-05

        def gelu_new(x):
            c = jnp.sqrt(jnp.asarray(2.0 / jnp.pi, x.dtype))
            return 0.5 * x * (1.0 + jnp.tanh(c * (x + 0.044715 * x * x * x)))
        key = jax.random.key(seed)
        ks = jax.random.split(key, 5)
        b, s = (2, 512)
        x = jax.random.normal(ks[0], (b, s, N_DIM), dtype=jnp.float32)
        w_q = jax.random.normal(ks[1], (N_DIM, 2 * H * KD), dtype=jnp.float32) * 0.02
        bn_gamma = jnp.ones((2 * H * KD,), dtype=jnp.float32)
        bn_beta = jnp.zeros((2 * H * KD,), dtype=jnp.float32)
        keys = jax.random.normal(ks[2], (H, NUM_KEYS, 2, KD), dtype=jnp.float32) * 0.02
        down_embed = jax.random.normal(ks[3], (N_EXPERTS, N_DIM), dtype=jnp.float32) * 0.02
        up_embed = jax.random.normal(ks[4], (N_EXPERTS, N_DIM), dtype=jnp.float32) * 0.02
        return {'x': x, 'w_q': w_q, 'bn_gamma': bn_gamma, 'bn_beta': bn_beta, 'keys': keys, 'down_embed': down_embed, 'up_embed': up_embed}
    _L0_ffn_all = _L0_ffn_setup()
    _L0_ffn_in = {k: v for k, v in _L0_ffn_all.items() if k in ('w_q', 'bn_gamma', 'bn_beta', 'keys', 'down_embed', 'up_embed')}
    del _L0_ffn_all
    return {'x': x, 'ctx_1024': ctx_1024, 'mask_1x1xSxS2_fk0': mask_1x1xSxS2_fk0, 'L0_attn_qkv_w': _L0_attn_in['qkv_w'], 'L0_attn_proj_w': _L0_attn_in['proj_w'], 'L0_attn_proj_b': _L0_attn_in['proj_b'], 'L0_attn_curvature': _L0_attn_in['curvature'], 'L0_xattn_Wq': _L0_xattn_in['Wq'], 'L0_xattn_bq': _L0_xattn_in['bq'], 'L0_xattn_Wk': _L0_xattn_in['Wk'], 'L0_xattn_bk': _L0_xattn_in['bk'], 'L0_xattn_Wv': _L0_xattn_in['Wv'], 'L0_xattn_bv': _L0_xattn_in['bv'], 'L0_xattn_Wo': _L0_xattn_in['Wo'], 'L0_xattn_bo': _L0_xattn_in['bo'], 'L0_ffn_w_q': _L0_ffn_in['w_q'], 'L0_ffn_bn_gamma': _L0_ffn_in['bn_gamma'], 'L0_ffn_bn_beta': _L0_ffn_in['bn_beta'], 'L0_ffn_keys': _L0_ffn_in['keys'], 'L0_ffn_down_embed': _L0_ffn_in['down_embed'], 'L0_ffn_up_embed': _L0_ffn_in['up_embed']}

def reference(x, ctx_1024, mask_1x1xSxS2_fk0, L0_attn_qkv_w, L0_attn_proj_w, L0_attn_proj_b, L0_attn_curvature, L0_xattn_Wq, L0_xattn_bq, L0_xattn_Wk, L0_xattn_bk, L0_xattn_Wv, L0_xattn_bv, L0_xattn_Wo, L0_xattn_bo, L0_ffn_w_q, L0_ffn_bn_gamma, L0_ffn_bn_beta, L0_ffn_keys, L0_ffn_down_embed, L0_ffn_up_embed):
    import jax
    import jax.numpy as jnp

    def _L0_attn_ref(x, qkv_w, proj_w, proj_b, curvature):
        import math
        import jax, jax.numpy as jnp
        import numpy as np
        B, T, C = (2, 1024, 512)
        H, N1, N2, N3 = (16, 6, 4, 6)
        HD = C // H

        def _rotary(T_, hd, dtype):
            inv_freq = 1.0 / 10000.0 ** (jnp.arange(0, hd, 2, dtype=jnp.float32) / hd)
            freqs = jnp.outer(jnp.arange(T_, dtype=jnp.float32), inv_freq)
            return (jnp.cos(freqs)[None, :, None, :].astype(dtype), jnp.sin(freqs)[None, :, None, :].astype(dtype))

        def _apply_rot(x, cos, sin):
            x1, x2 = (x[..., :x.shape[-1] // 2], x[..., x.shape[-1] // 2:])
            return jnp.concatenate([x1 * cos + x2 * sin, -x1 * sin + x2 * cos], axis=-1).astype(x.dtype)

        def _causal_bias(L, S, dtype):
            mask = jnp.triu(jnp.ones((L, S), bool), k=1)
            return jnp.where(mask, jnp.asarray(-jnp.inf, dtype), jnp.asarray(0.0, dtype))

        def _sdpa(q, k, v, scale):
            scores = jnp.einsum('bhtd,bhsd->bhts', q, k) * scale + _causal_bias(q.shape[-2], k.shape[-2], q.dtype)
            return jnp.einsum('bhts,bhsd->bhtd', jax.nn.softmax(scores, axis=-1), v)

        def _hyp_attn(q, k, v, curv):
            eps = 1e-06
            tq = jnp.sqrt(1.0 / curv + jnp.sum(q * q, axis=-1, keepdims=True))
            tk = jnp.sqrt(1.0 / curv + jnp.sum(k * k, axis=-1, keepdims=True))
            inner = jnp.einsum('bhtd,bhsd->bhts', q, k) - tq * jnp.swapaxes(tk, -1, -2)
            arg = jnp.maximum(-curv * inner, 1.0 + 1e-07)
            dis = jnp.sqrt(1.0 / curv) * jnp.arccosh(arg)
            scores = 1.0 / (eps + dis) + _causal_bias(q.shape[-2], k.shape[-2], q.dtype)
            return jnp.einsum('bhts,bhsd->bhtd', jax.nn.softmax(scores, axis=-1), v)
        Bx, Tx, Cx = x.shape
        qkv = x @ qkv_w.T
        q, k, v = jnp.split(qkv, 3, axis=-1)
        q = q.reshape(Bx, Tx, H, HD)
        k = k.reshape(Bx, Tx, H, HD)
        v = v.reshape(Bx, Tx, H, HD)
        cos, sin = _rotary(Tx, HD, x.dtype)
        q = _apply_rot(q, cos, sin)
        k = _apply_rot(k, cos, sin)
        q, k, v = (jnp.swapaxes(t, 1, 2) for t in (q, k, v))
        outs = []
        outs.append(_sdpa(q[:, :N1], k[:, :N1], v[:, :N1], 1.0 / math.sqrt(HD)))
        outs.append(_hyp_attn(q[:, N1:N1 + N2], k[:, N1:N1 + N2], v[:, N1:N1 + N2], curvature))
        qn = q[:, N1 + N2:] / jnp.maximum(jnp.linalg.norm(q[:, N1 + N2:], axis=-1, keepdims=True), 1e-12)
        kn = k[:, N1 + N2:] / jnp.maximum(jnp.linalg.norm(k[:, N1 + N2:], axis=-1, keepdims=True), 1e-12)
        outs.append(_sdpa(qn, kn, v[:, N1 + N2:], math.sqrt(HD)))
        y = jnp.concatenate(outs, axis=1)
        y = jnp.swapaxes(y, 1, 2).reshape(Bx, Tx, Cx)
        return y @ proj_w.T + proj_b

    def _L0_xattn_ref(x, y, mask, Wq, bq, Wk, bk, Wv, bv, Wo, bo, num_heads):
        import jax, jax.numpy as jnp
        import numpy as np
        B, T, E, H = (2, 1024, 512, 16)
        Bx, Tq, Emb = x.shape
        Tkv = y.shape[1]
        d = Emb // num_heads
        q = (x @ Wq + bq).reshape(Bx, Tq, num_heads, d)
        k = (y @ Wk + bk).reshape(Bx, Tkv, num_heads, d)
        v = (y @ Wv + bv).reshape(Bx, Tkv, num_heads, d)
        scale = 1.0 / np.sqrt(d).astype(np.float32)
        att = scale * jnp.einsum('bthd,bThd->bhtT', q, k)
        att = att * mask - 10000000000.0 * (1.0 - mask)
        att = jax.nn.softmax(att, axis=-1)
        out = jnp.einsum('bhtT,bThd->bthd', att, v).reshape(Bx, Tq, Emb)
        return out @ Wo + bo

    def _L0_ffn_ref(x, w_q, bn_gamma, bn_beta, keys, down_embed, up_embed):
        import jax, jax.numpy as jnp
        import numpy as np
        H = 8
        KD = 128
        TOPK = 8
        NUM_KEYS = 128
        N_EXPERTS = NUM_KEYS * NUM_KEYS
        N_DIM = 512
        BN_EPS = 1e-05

        def gelu_new(x):
            c = jnp.sqrt(jnp.asarray(2.0 / jnp.pi, x.dtype))
            return 0.5 * x * (1.0 + jnp.tanh(c * (x + 0.044715 * x * x * x)))
        b, n, d = x.shape
        q = jnp.einsum('bnd,de->bne', x, w_q)
        mean = jnp.mean(q, axis=(0, 1))
        var = jnp.var(q, axis=(0, 1))
        q = (q - mean) * jax.lax.rsqrt(var + BN_EPS) * bn_gamma + bn_beta
        q = q.reshape(b, n, 2, H, KD).transpose(2, 0, 1, 3, 4)
        sim = jnp.einsum('pbnhd,hkpd->pbnhk', q, keys)
        sx, ix = jax.lax.top_k(sim[0], TOPK)
        sy, iy = jax.lax.top_k(sim[1], TOPK)
        all_scores = (sx[..., :, None] + sy[..., None, :]).reshape(b, n, H, TOPK * TOPK)
        all_indices = (ix[..., :, None] * NUM_KEYS + iy[..., None, :]).reshape(b, n, H, TOPK * TOPK)
        scores, pk = jax.lax.top_k(all_scores, TOPK)
        indices = jnp.take_along_axis(all_indices, pk, axis=-1)
        wd = down_embed[indices]
        wu = up_embed[indices]
        h = jnp.einsum('bnd,bnhkd->bnhk', x, wd)
        h = gelu_new(h)
        h = jax.nn.softmax(scores, axis=-1) * h
        out = jnp.einsum('bnhk,bnhkd->bnd', h, wu)
        return out
    x = x + _L0_attn_ref(_layernorm(x, axis=-1), L0_attn_qkv_w, L0_attn_proj_w, L0_attn_proj_b, L0_attn_curvature)
    x = x + _L0_xattn_ref(_layernorm(x, axis=-1), ctx_1024, mask_1x1xSxS2_fk0, L0_xattn_Wq, L0_xattn_bq, L0_xattn_Wk, L0_xattn_bk, L0_xattn_Wv, L0_xattn_bv, L0_xattn_Wo, L0_xattn_bo, 16)
    x = x + _L0_ffn_ref(_layernorm(x, axis=-1), L0_ffn_w_q, L0_ffn_bn_gamma, L0_ffn_bn_beta, L0_ffn_keys, L0_ffn_down_embed, L0_ffn_up_embed)
    return x

_drawn_inputs = setup_inputs


def setup_inputs(seed=0):
    import zlib

    import numpy as np

    out = dict(_drawn_inputs(seed))
    spreads = {'L0_attn_proj_b': (0.0, 0.1),
     'L0_attn_curvature': (1.0, 0.6),
     'L0_xattn_bq': (0.0, 0.343),
     'L0_xattn_bk': (0.0, 0.8),
     'L0_xattn_bv': (0.0, 0.1),
     'L0_xattn_bo': (0.0, 0.1),
     'L0_ffn_bn_gamma': (1.0, 0.6),
     'L0_ffn_bn_beta': (0.0, 0.8)}
    factors = {'L0_ffn_w_q': 8.0, 'L0_ffn_keys': 8.0, 'L0_ffn_down_embed': 8.0, 'L0_ffn_up_embed': 8.0}
    for name, (base, spread) in spreads.items():
        noise = np.random.default_rng([zlib.crc32(name.encode()), seed]).standard_normal(out[name].shape)
        drawn = base * np.exp(spread * noise) if base else spread * noise
        out[name] = jnp.asarray(drawn.astype(out[name].dtype))
    for name, factor in factors.items():
        out[name] = (out[name] * factor).astype(out[name].dtype)
    return out
```

```python
from contextlib import ExitStack

import concourse.bass as bass
from concourse import mybir

F32 = mybir.dt.float32
U32 = mybir.dt.uint32
ALU = mybir.AluOpType
ACT = mybir.ActivationFunctionType
AX_X = mybir.AxisListType.X

B, S, D = 8, 224, 512
SC = 750
H, HD = 16, 32
N_SDPA, N_HYP, N_COS = 6, 4, 6
N_DOT = N_SDPA + N_COS
HEADS = (*range(N_SDPA), *range(N_SDPA + N_HYP, H), *range(N_SDPA, N_SDPA + N_HYP))
P = 128
KC = D // P
TT = 112
NT = S // TT
CT, NC = 125, SC // 125
HC = SC // 2
HB = 3 * TT
NU = NT * H
HYW = TT + S
LN_EPS = 1e-5
NEG = -3.0e38

SQRT_HD = float(HD) ** 0.5


def spread(ap, axis, n):
    ap = ap.unsqueeze(axis)
    shape = list(ap.shape)
    shape[axis] = n
    return ap.to_broadcast(shape)


class Steps:

    def __init__(self, sem, per):
        self.sem, self.per = sem, per

    def at(self, b, n):
        return b * self.per + n


def self_units():
    return ([(t, h) for t in range(NT) for h in range(N_DOT)]
            + [(t, h) for t in range(NT) for h in range(N_DOT, H)])


UNITS = self_units()
N_SDOT = NT * N_DOT
V_SELF, V_FROM = 4, 4
ROOT_AT, LN_AT = 8, 13


def build_attention(nc, a, x2_dram):
    with ExitStack() as ctx:
        def sb(name, shape, dt=F32):
            return ctx.enter_context(nc.sbuf_tensor(name, shape, dt))

        def psum(name, shape):
            return ctx.enter_context(nc.psum_tensor(name, shape, F32))

        def sem(name):
            return ctx.enter_context(nc.semaphore(name))

        def steps(name, per):
            return Steps(sem(name), per)

        w_qkv = sb("w_qkv", [P, KC, 3 * D])
        w_proj = sb("w_proj", [P, KC, D])
        w_q = sb("w_q", [P, KC, D])
        w_k = sb("w_k", [P, KC, D])
        w_v = sb("w_v", [P, KC, D])
        w_o = sb("w_o", [P, KC, D])
        proj_b = sb("proj_b", [P, D])
        bv = sb("bv", [P, D])
        bo = sb("bo", [P, D])
        bq = sb("bq", [P, KC])
        bk = sb("bk", [P, KC])
        rot_cos = sb("rot_cos", [TT, NT, HD])
        rot_sin = sb("rot_sin", [TT, NT, HD])
        curv = sb("curv", [P, N_HYP])
        mask = sb("mask", [TT, NT, SC])
        mask_bias = sb("mask_bias", [TT, NT, SC])
        ident = sb("ident", [P, P])
        causal = sb("causal", [TT, HYW])
        half = sb("half", [TT, 40])
        minus_half = sb("minus_half", [TT, NT])
        neg_curv = sb("neg_curv", [P, N_HYP])
        inv_curv = sb("inv_curv", [P, N_HYP])
        root_inv_curv = sb("root_inv_curv", [P, N_HYP])
        norm_add = sb("norm_add", [TT, N_COS + N_HYP])
        factor = sb("factor", [TT, 2 * NT, H])

        x_in = sb("x_in", [TT, NT, D])
        ctx_t = sb("ctx_t", [P, KC, SC])
        k_t = sb("k_t", [P, KC, SC])
        v_c = sb("v_c", [CT, NC, D])
        x_b = sb("x_b", [TT, NT, D])
        x_n = sb("x_n", [TT, NT, D])
        act_t = sb("act_t", [P, KC, S])
        stats = sb("stats", [TT, NT, 6])
        mean_var = sb("mean_var", [TT, NT, 2])
        var_eps = sb("var_eps", [TT, NT])
        rstd = sb("rstd", [TT, NT])
        qk = sb("qk", [TT, 2 * NT, D + P])
        sums = sb("sums", [TT, 2 * NT, N_COS + N_HYP])
        norms = sb("norms", [TT, 2 * NT, N_COS + N_HYP])
        v_s = sb("v_s", [TT, NT, D])
        keys_t = sb("keys_t", [P, KC + 1, S])
        q_m = sb("q_m", [P, H + N_HYP, S])
        neg_s = sb("neg_s", [TT, 3, SC])
        neg_max = sb("neg_max", [TT, NU])
        prob = sb("prob", [TT, 3, SC])
        room = prob[:].rearrange("p i n -> p (i n)")
        rot_a = room[:, 0:2 * D].rearrange("p (i n) -> p i n", i=2)
        rot_b = room[:, 2 * D:4 * D].rearrange("p (i n) -> p i n", i=2)
        squares = neg_s[:, 0:2, 0:(N_COS + N_HYP) * HD]
        arg = neg_s[:, :, S:S + N_HYP * TT]
        hyp = qk[:, 0:3, 0:N_HYP * TT]
        prob_t = sb("prob_t", [P, 2, 2 * HB])
        row_sum = sb("row_sum", [TT, NU])
        inv_sum = sb("inv_sum", [NU, TT])
        head_rows = sb("head_rows", [NU, NT * KC, P])
        x1 = sb("x1", [TT, NT, D])
        x2 = x1
        inv_spread = keys_t[:].rearrange("p c s -> p (c s)")[:, 0:NT * KC * TT].rearrange("p (t n) -> p t n", t=NT)

        ps_s = [psum(f"ps_s{i}", [P, 2, 512]) for i in range(2)]
        bank = [ps_s[0][:, 0, :], ps_s[0][:, 1, :], ps_s[1][:, 0, :], ps_s[1][:, 1, :]]
        ps_t = [psum(f"ps_t{i}", [P, 512]) for i in range(2)]
        ps_o = [psum(f"ps_o{i}", [P, 512]) for i in range(2)]

        def hyp_part(blocks, t, hh):
            return blocks[:, t:2 * t + 1, hh * TT:(hh + 1) * TT]

        def by_tile(ap):
            return ap.rearrange("p (k n) -> p k n", n=TT)

        passed_dve = sem("passed_dve")
        passed_pool = sem("passed_pool")
        weights_in = sem("weights_in")
        tables_in = sem("tables_in")
        x_loaded = steps("x_loaded", 16)
        ctx_loaded = steps("ctx_loaded", 16)
        consts = sem("consts")
        pool_consts = sem("pool_consts")
        var_ready = steps("var_ready", 2)
        rstd_ready = steps("rstd_ready", 2)
        xn_ready = steps("xn_ready", 2 * NT)
        xb_ready = steps("xb_ready", 1)
        act_tr = steps("act_tr", 2 * NT)
        act_ready = steps("act_ready", 4 * NT)
        k_done = steps("k_done", 2 * KC)
        k_ready = steps("k_ready", 2 * KC)
        qkv_done = steps("qkv_done", 3 * NT)
        rot_parts = steps("rot_parts", 2 * NT)
        rot_ready = steps("rot_ready", 2 * NT)
        vs_ready = steps("vs_ready", NT)
        sq_ready = steps("sq_ready", 2 * NT)
        sq_used = steps("sq_used", 2 * NT)
        sums_ready = steps("sums_ready", 1)
        norms_ready = steps("norms_ready", 1)
        qk_scaled = steps("qk_scaled", 2 * NT)
        qk_tr = steps("qk_tr", 3 * NT)
        q_turned = steps("q_turned", 2 * NT)
        k_turned = steps("k_turned", NT)
        hyp_done = steps("hyp_done", N_HYP * NT)
        arg_ready = steps("arg_ready", N_HYP * NT)
        arg1_ready = steps("arg1_ready", 1)
        hyp_sq_ready = steps("hyp_sq_ready", 1)
        hyp_root_ready = steps("hyp_root_ready", 1)
        hyp_sum_ready = steps("hyp_sum_ready", 1)
        hyp_ln_ready = steps("hyp_ln_ready", 1)
        hyp_scaled = steps("hyp_scaled", 1)
        s_done = steps("s_done", N_SDOT)
        s_shifted = steps("s_shifted", NU)
        p_ready = steps("p_ready", NU)
        p_tr = steps("p_tr", NU)
        pt_ready = steps("pt_ready", NU)
        pv_done = steps("pv_done", NU)
        sum_tr = steps("sum_tr", 2)
        inv_ready = steps("inv_ready", 2)
        inv_spread_done = steps("inv_spread_done", 2 * NT)
        proj_done = steps("proj_done", 2 * NT)
        x1_ready = steps("x1_ready", NT)
        x1b_ready = steps("x1b_ready", 1)
        v_done = steps("v_done", NC)
        v_ready = steps("v_ready", NC)
        q2_done = steps("q2_done", KC)
        q2_ready = [steps(f"q2_ready{i}", KC // 2) for i in range(2)]
        cs_done = steps("cs_done", NU)
        cs_masked = steps("cs_masked", NU)
        cs_shifted = steps("cs_shifted", NU)
        cp_ready = steps("cp_ready", NU)
        cp_tr = steps("cp_tr", 2 * NU)
        cpt_ready = steps("cpt_ready", 2 * NU)
        cpv_done = steps("cpv_done", NU)
        x2_ready = steps("x2_ready", NT)
        x2_stored = steps("x2_stored", 16)

        def out_t(t, h):
            return ps_o[t][HD * (h % 4):HD * (h % 4 + 1), (h // 4) * TT:(h // 4 + 1) * TT]

        x_v = a["x"].rearrange("b (t p) d -> b p t d", p=TT)
        x2_v = x2_dram.rearrange("(b t p) d -> b p t d", p=TT, t=NT)
        ctx_v = a["ctx_t"].rearrange("b (c p) s -> b p c s", p=P)

        def batch_of(view, b):
            return view[bass.ds(b, 1)].rearrange("o p t d -> (o p) t d")

        block = ctx.enter_context(nc.Block())

        @block.sync
        def _(sp):
            def weight(dst, src):
                sp.dma_start(dst[:], src.rearrange("(c p) n -> p c n", p=P)).then_inc(weights_in, 16)

            sp.dma_start(x_in[:], batch_of(x_v, 0)).then_inc(x_loaded.sem, 16)
            sp.dma_start(ctx_t[:], batch_of(ctx_v, 0)).then_inc(ctx_loaded.sem, 16)
            for dst, src in ((w_k, "wk"), (w_qkv, "w_qkv_t"), (w_v, "wv"), (w_proj, "w_proj_t"), (w_q, "wq"),
                             (w_o, "wo")):
                weight(dst, a[src])
            with sp.Fori(0, B - 1) as b:
                sp.wait_ge(xb_ready.sem, xb_ready.at(b, 1))
                sp.wait_ge(xn_ready.sem, xn_ready.at(b, NT))
                sp.dma_start(x_in[:], batch_of(x_v, b + 1)).then_inc(x_loaded.sem, 16)
                sp.wait_ge(v_done.sem, v_done.at(b, NC))
                sp.dma_start(ctx_t[:], batch_of(ctx_v, b + 1)).then_inc(ctx_loaded.sem, 16)

        @block.tensor
        def _(pe):
            def k_group(b, g, n):
                c, part = g // 2, g % 2
                for kc in range(KC):
                    mm = nc.tensor.matmul(bank[n % 4][:, 0:HC], w_k[:, kc, c * P:(c + 1) * P],
                                          ctx_t[:, kc, part * HC:(part + 1) * HC],
                                          start=(kc == 0), stop=(kc == KC - 1))
                mm.then_inc(k_done.sem, 1)

            def act_transpose(b, t):
                for c in range(KC):
                    mm = nc.tensor.transpose(ps_t[t][:, c * TT:(c + 1) * TT], x_n[:, t, c * P:(c + 1) * P],
                                             ident[0:TT, 0:TT])
                mm.then_inc(act_tr.sem, 1)

            def spread_sums(b, k):
                pe.wait_ge(inv_ready.sem, inv_ready.at(b, k + 1))
                for t in range(NT):
                    for c in range(KC):
                        mm = nc.tensor.matmul(ps_t[t][:, c * TT:(c + 1) * TT], head_rows[:, t * KC + c, :], inv_sum[:],
                                              start=True, stop=True)
                    mm.then_inc(inv_spread_done.sem, 1)

            def project(out, w, t, done):
                for kc in range(KC):
                    mm = nc.tensor.matmul(out[0:TT, :], act_t[:, kc, t * TT:(t + 1) * TT], w[:, kc, :],
                                          start=(kc == 0), stop=(kc == KC - 1))
                mm.then_inc(done.sem, 1)

            def v_step(b, m):
                j, kc = m // KC, m % KC
                if kc == 0:
                    if j < 2:
                        pe.wait_ge(arg_ready.sem, arg_ready.at(b, N_HYP * NT))
                    else:
                        pe.wait_ge(v_ready.sem, v_ready.at(b, j - 1))
                mm = nc.tensor.matmul(bank[2 + j % 2][0:CT, :], ctx_t[:, kc, j * CT:(j + 1) * CT], w_v[:, kc, :],
                                      start=(kc == 0), stop=(kc == KC - 1))
                if kc == KC - 1:
                    mm.then_inc(v_done.sem, 1)

            pe.wait_ge(weights_in, 16 * 6)
            pe.wait_ge(pool_consts, 3)
            with pe.Fori(0, B) as b:
                pe.wait_ge(ctx_loaded.sem, ctx_loaded.at(b, 16))
                for g in range(4):
                    k_group(b, g, g)
                for t in range(NT):
                    pe.wait_ge(xn_ready.sem, xn_ready.at(b, t + 1))
                    act_transpose(b, t)
                for j in range(3 * NT):
                    t, part = j // 3, j % 3
                    if part == 0:
                        pe.wait_ge(act_ready.sem, act_ready.at(b, t + 1))
                    if j < 4:
                        pe.wait_ge(k_ready.sem, k_ready.at(b, j + 1))
                    else:
                        pe.wait_ge(rot_parts.sem, rot_parts.at(b, j - 3))
                    for kc in range(KC):
                        mm = nc.tensor.matmul(bank[j % 4][0:TT, :], act_t[:, kc, t * TT:(t + 1) * TT],
                                              w_qkv[:, kc, part * D:(part + 1) * D],
                                              start=(kc == 0), stop=(kc == KC - 1))
                    mm.then_inc(qkv_done.sem, 1)
                for g, last in zip(range(4, 8), ((vs_ready, 1), (rot_parts, 3), (rot_parts, 4), (vs_ready, 2))):
                    pe.wait_ge(last[0].sem, last[0].at(b, last[1]))
                    k_group(b, g, g + 2)
                for g in range(3 * NT):
                    t, r = g // 3, g % 3
                    pe.wait_ge(qk_scaled.sem, qk_scaled.at(b, 2 * t + min(r, 1) + 1))
                    if g >= 2:
                        t0, r0 = (g - 2) // 3, (g - 2) % 3
                        if r0 == 1:
                            pe.wait_ge(k_turned.sem, k_turned.at(b, t0 + 1))
                        else:
                            pe.wait_ge(q_turned.sem, q_turned.at(b, 2 * t0 + r0 // 2 + 1))
                    for c in range(KC if r < 2 else 2):
                        src = qk[:, 2 * t + r, c * P:(c + 1) * P] if r < 2 else qk[:, 2 * t + c, D:D + P]
                        mm = nc.tensor.transpose(ps_t[g % 2][:, c * TT:(c + 1) * TT], src, ident[0:TT, 0:TT])
                    mm.then_inc(qk_tr.sem, 1)
                pe.wait_ge(q_turned.sem, q_turned.at(b, 2 * NT))
                pe.wait_ge(k_turned.sem, k_turned.at(b, NT))
                pe.wait_ge(k_ready.sem, k_ready.at(b, 2 * KC))
                for g in range(N_HYP * NT):
                    t, hh = g // N_HYP, g % N_HYP
                    nk = (t + 1) * TT
                    if g >= N_HYP:
                        pe.wait_ge(arg_ready.sem, arg_ready.at(b, g - N_HYP + 1))
                    for c in (KC - 1, KC):
                        mm = nc.tensor.matmul(bank[hh][0:TT, 0:nk], q_m[:, 4 * c + hh, t * TT:(t + 1) * TT],
                                              keys_t[:, c, 0:nk], start=(c == KC - 1), stop=(c == KC))
                    mm.then_inc(hyp_done.sem, 1)

                def scores(u):
                    t, h = UNITS[u]
                    nk = (t + 1) * TT
                    if u < 2:
                        pe.wait_ge(arg_ready.sem, arg_ready.at(b, N_HYP + u + 1))
                    else:
                        pe.wait_ge(s_shifted.sem, s_shifted.at(b, u - 1))
                    nc.tensor.matmul(bank[u % 2][0:TT, 0:nk], q_m[:, h, t * TT:(t + 1) * TT],
                                     keys_t[:, h // 4, 0:nk], start=True, stop=True).then_inc(s_done.sem, 1)

                def turn(u):
                    t, h = UNITS[u]
                    pe.wait_ge(p_ready.sem, p_ready.at(b, u + 1))
                    if u >= 2:
                        pe.wait_ge(pt_ready.sem, pt_ready.at(b, u - 1))
                    for j in range(t + 1):
                        mm = nc.tensor.transpose(ps_t[u % 2][0:TT, j * TT:(j + 1) * TT],
                                                 prob[:, u % 3, j * TT:(j + 1) * TT], ident[0:TT, 0:TT])
                    mm.then_inc(p_tr.sem, 1)

                def weigh(u):
                    t, h = UNITS[u]
                    pe.wait_ge(pt_ready.sem, pt_ready.at(b, u + 1))
                    for j in range(t + 1):
                        mm = nc.tensor.matmul(out_t(t, h), v_s[:, j, h * HD:(h + 1) * HD],
                                              prob_t[0:TT, u % 2, j * TT:(j + 1) * TT], start=(j == 0), stop=(j == t))
                    mm.then_inc(pv_done.sem, 1)

                pe.wait_ge(vs_ready.sem, vs_ready.at(b, NT))
                for u in range(NU + 4):
                    if u < N_SDOT:
                        scores(u)
                    if 3 <= u < NU + 3:
                        turn(u - 3)
                    if V_FROM <= u < V_FROM + KC * V_SELF:
                        v_step(b, u - V_FROM)
                    if u >= 4:
                        weigh(u - 4)
                pe.wait_ge(p_ready.sem, p_ready.at(b, NU))
                nc.tensor.transpose(ps_t[0][0:NU, 0:TT], row_sum[:], ident[0:TT, 0:TT]).then_inc(sum_tr.sem, 1)
                for m in range(KC * V_SELF, KC * (V_SELF + 1)):
                    v_step(b, m)
                spread_sums(b, 0)
                for t in range(NT):
                    pe.wait_ge(act_ready.sem, act_ready.at(b, NT + t + 1))
                    project(ps_o[t], w_proj, t, proj_done)
                for m in range(KC * (V_SELF + 1), KC * NC):
                    v_step(b, m)
                for t in range(NT):
                    pe.wait_ge(xn_ready.sem, xn_ready.at(b, NT + t + 1))
                    act_transpose(b, t)
                pe.wait_ge(act_ready.sem, act_ready.at(b, 3 * NT))
                pe.wait_ge(v_ready.sem, v_ready.at(b, NC))
                for c in range(KC):
                    for kc in range(KC):
                        mm = nc.tensor.matmul(bank[c][:, 0:S], w_q[:, kc, c * P:(c + 1) * P], act_t[:, kc, :],
                                              start=(kc == 0), stop=(kc == KC - 1))
                    mm.then_inc(q2_done.sem, 1)

                def cross_scores(u):
                    t, h = u // H, u % H
                    if u >= 2:
                        pe.wait_ge(cs_masked.sem, cs_masked.at(b, u - 1))
                    for part in range(2):
                        mm = nc.tensor.matmul(ps_s[u % 2][0:TT, part, 0:HC], q_m[:, h, t * TT:(t + 1) * TT],
                                              k_t[:, h // 4, part * HC:(part + 1) * HC], start=True, stop=True)
                    mm.then_inc(cs_done.sem, 1)

                def cross_turn(u):
                    pe.wait_ge(cp_ready.sem, cp_ready.at(b, u + 1))
                    for i in range(2):
                        if u >= 1:
                            pe.wait_ge(cpt_ready.sem, cpt_ready.at(b, 2 * u - 1 + i))
                        for j in range(3):
                            o = (3 * i + j) * CT
                            mm = nc.tensor.transpose(ps_t[i][0:CT, j * TT:(j + 1) * TT], prob[:, u % 3, o:o + CT],
                                                     ident[0:TT, 0:TT])
                        mm.then_inc(cp_tr.sem, 1)

                def cross_weigh(u):
                    t, h = u // H, u % H
                    for j in range(NC):
                        if j % 3 == 0:
                            pe.wait_ge(cpt_ready.sem, cpt_ready.at(b, 2 * u + j // 3 + 1))
                        mm = nc.tensor.matmul(out_t(t, h), v_c[:, j, h * HD:(h + 1) * HD],
                                              prob_t[0:CT, u % 2, j * TT:(j + 1) * TT], start=(j == 0),
                                              stop=(j == NC - 1))
                    mm.then_inc(cpv_done.sem, 1)

                for ready in q2_ready:
                    pe.wait_ge(ready.sem, ready.at(b, KC // 2))
                for u in range(NU + 3):
                    if u < NU:
                        cross_scores(u)
                    if 2 <= u < NU + 2:
                        cross_turn(u - 2)
                    if u >= 3:
                        cross_weigh(u - 3)
                nc.tensor.transpose(ps_t[0][0:NU, 0:TT], row_sum[:], ident[0:TT, 0:TT]).then_inc(sum_tr.sem, 1)
                spread_sums(b, 1)
                for t in range(NT):
                    pe.wait_ge(act_ready.sem, act_ready.at(b, 3 * NT + t + 1))
                    project(ps_o[t], w_o, t, proj_done)

        @block.vector
        def _(dve):
            dve.wait_ge(tables_in, 16 * 9)
            nc.vector.tensor_scalar(mask_bias[:], mask[:], -1.0, 1.0, ALU.mult, ALU.add)
            nc.vector.memset(factor[:], 1.0)
            nc.vector.memset(qk[:], 0.0)
            nc.vector.memset(half[:], 0.5)
            nc.vector.memset(minus_half[:], -0.5)
            nc.vector.memset(norm_add[:], 0.0)
            nc.vector.tensor_scalar(neg_curv[:], curv[:], -1.0, None, ALU.mult)
            nc.vector.reciprocal(inv_curv[:], curv[:])
            nc.vector.drain()
            nc.vector.tensor_scalar(mask_bias[:], mask_bias[:], -1.0e10, None, ALU.mult)
            nc.vector.tensor_copy(norm_add[:, N_COS:], inv_curv[0:TT, :])
            nc.vector.memset(factor[:, 0:2 * NT:2, 0:N_SDPA], 1.0 / SQRT_HD)
            nc.vector.drain().then_inc(consts, 1)

            def norm(b, src, k):
                for t in range(NT):
                    nc.vector.bn_stats(stats[:, t, :], src[:, t, :])
                nc.vector.drain()
                for t in range(NT):
                    nc.vector.bn_aggr(mean_var[:, t, :], stats[:, t, :])
                nc.vector.drain()
                nc.vector.tensor_scalar(var_eps[:], mean_var[:, :, 1], LN_EPS, None, ALU.add)\
                    .then_inc(var_ready.sem, 1)
                dve.wait_ge(rstd_ready.sem, rstd_ready.at(b, k + 1))
                for t in range(NT):
                    nc.vector.tensor_scalar(x_n[:, t, :], src[:, t, :], mean_var[:, t, 0:1], rstd[:, t:t + 1],
                                            ALU.subtract, ALU.mult).then_inc(xn_ready.sem, 1)

            def act_out(b, k, t):
                dve.wait_ge(act_tr.sem, act_tr.at(b, NT * k + t + 1))
                nc.vector.tensor_copy(act_t[:, :, t * TT:(t + 1) * TT],
                                      ps_t[t][:, 0:KC * TT].rearrange("p (c n) -> p c n", c=KC))\
                    .then_inc(act_ready.sem, 1)

            def v_out(b, j):
                dve.wait_ge(v_done.sem, v_done.at(b, j + 1))
                nc.vector.tensor_tensor(v_c[:, j, :], bank[2 + j % 2][0:CT, :], bv[0:CT, :], ALU.add)\
                    .then_inc(v_ready.sem, 1)

            def inverses(b, k):
                dve.wait_ge(sum_tr.sem, sum_tr.at(b, k + 1))
                nc.vector.reciprocal(inv_sum[:], ps_t[0][0:NU, 0:TT]).then_inc(inv_ready.sem, 1)

            def outputs(b, k):
                for t in range(NT):
                    dve.wait_ge(inv_spread_done.sem, inv_spread_done.at(b, NT * k + t + 1))
                    nc.vector.tensor_copy(inv_spread[:, t, :], ps_t[t][:, 0:KC * TT])
                nc.vector.drain()
                for t in range(NT):
                    nc.vector.tensor_tensor(act_t[:, :, t * TT:(t + 1) * TT],
                                            ps_o[t][:, 0:KC * TT].rearrange("p (c n) -> p c n", c=KC),
                                            inv_spread[:, t, :].rearrange("p (c n) -> p c n", c=KC), ALU.mult)\
                        .then_inc(act_ready.sem, 1)

            with dve.Fori(0, B) as b:
                dve.wait_ge(x_loaded.sem, x_loaded.at(b, 16))
                norm(b, x_in, 0)
                for t in range(NT):
                    act_out(b, 0, t)
                for r in range(2 * NT):
                    t, part = r // 2, r % 2
                    j = 3 * t + part
                    dve.wait_ge(qkv_done.sem, qkv_done.at(b, j + 1))
                    if r >= 2:
                        dve.wait_ge(rot_ready.sem, rot_ready.at(b, r - 1))
                    src = bank[j % 4][0:TT, :].rearrange("p (h s d) -> p h s d", h=H, s=2)
                    parts = rot_b[:, part, :].rearrange("p (h s d) -> p h s d", h=H, s=2)
                    nc.vector.tensor_tensor(rot_a[:, part, :].rearrange("p (h d) -> p h d", h=H),
                                            bank[j % 4][0:TT, :].rearrange("p (h d) -> p h d", h=H),
                                            spread(rot_cos[:, t, :], 1, H), ALU.mult)
                    for s in range(2):
                        last = nc.vector.tensor_tensor(parts[:, :, s, :], src[:, :, 1 - s, :],
                                                       spread(rot_sin[:, t, s * HD // 2:(s + 1) * HD // 2], 1, H),
                                                       ALU.mult)
                    last.then_inc(rot_parts.sem, 1)
                for r in range(2 * NT):
                    dve.wait_ge(sq_ready.sem, sq_ready.at(b, r + 1))
                    nc.vector.tensor_reduce(sums[:, r, :], squares[:, r % 2, :].rearrange("p (h d) -> p h d", d=HD),
                                            AX_X, ALU.add).then_inc(sq_used.sem, 1)
                nc.vector.drain()
                nc.vector.tensor_tensor(sums[:], sums[:], spread(norm_add[:], 1, 2 * NT), ALU.add)\
                    .then_inc(sums_ready.sem, 1)
                dve.wait_ge(norms_ready.sem, norms_ready.at(b, 1))
                nc.vector.tensor_scalar(sums[:, :, 0:N_COS], norms[:, :, 0:N_COS], 1e-12, None, ALU.max)
                times = qk[:, :, D:].rearrange("p r (h d) -> p r h d", d=HD)
                nc.vector.tensor_copy(times[:, 0:2 * NT:2, :, 0], norms[:, 0:2 * NT:2, N_COS:])
                nc.vector.tensor_scalar(times[:, 1:2 * NT:2, :, 0], norms[:, 1:2 * NT:2, N_COS:], -1.0, None, ALU.mult)
                nc.vector.drain()
                nc.vector.reciprocal(factor[:, :, N_SDPA:N_DOT], sums[:, :, 0:N_COS])
                nc.vector.drain()
                nc.vector.tensor_scalar(factor[:, 0:2 * NT:2, N_SDPA:N_DOT], factor[:, 0:2 * NT:2, N_SDPA:N_DOT],
                                        SQRT_HD, None, ALU.mult)
                nc.vector.drain()
                for r in range(2 * NT):
                    view = qk[:, r, 0:D].rearrange("p (h d) -> p h d", h=H)
                    nc.vector.tensor_tensor(view, view, spread(factor[:, r, :], 2, HD), ALU.mult)\
                        .then_inc(qk_scaled.sem, 1)
                for t in range(NT):
                    dve.wait_ge(qk_tr.sem, qk_tr.at(b, 3 * t + 2))
                    nc.vector.tensor_copy(keys_t[:, 0:KC, t * TT:(t + 1) * TT],
                                          ps_t[(3 * t + 1) % 2][:, 0:KC * TT].rearrange("p (c n) -> p c n", n=TT))\
                        .then_inc(k_turned.sem, 1)
                for g in range(N_HYP * NT):
                    t, hh = g // N_HYP, g % N_HYP
                    nk = (t + 1) * TT
                    dve.wait_ge(hyp_done.sem, hyp_done.at(b, g + 1))
                    nc.vector.tensor_scalar(hyp_part(arg, t, hh), by_tile(bank[hh][0:TT, 0:nk]),
                                            neg_curv[0:TT, hh:hh + 1], 1.0 + 1e-7, ALU.mult, ALU.max)\
                        .then_inc(arg_ready.sem, 1)

                def shift(u):
                    t, h = UNITS[u]
                    nk, off = (t + 1) * TT, t * TT
                    if u < N_SDOT:
                        dve.wait_ge(s_done.sem, s_done.at(b, u + 1))
                        src = by_tile(bank[u % 2][0:TT, 0:nk])
                    else:
                        src = hyp_part(hyp, t, h - N_DOT)
                    if u >= 3:
                        dve.wait_ge(p_ready.sem, p_ready.at(b, u - 2))
                    dve.sem_inc(passed_dve, 1)
                    nc.vector.tensor_tensor_reduce(by_tile(neg_s[:, u % 3, 0:nk]), src,
                                                   by_tile(causal[:, off:off + nk]), -1.0, 3.4e38,
                                                   ALU.add, ALU.min, neg_max[:, u:u + 1]).then_inc(s_shifted.sem, 1)

                def turned(u):
                    t, h = UNITS[u]
                    nk = (t + 1) * TT
                    dve.wait_ge(p_tr.sem, p_tr.at(b, u + 1))
                    if u >= 2:
                        dve.wait_ge(pv_done.sem, pv_done.at(b, u - 1))
                    nc.vector.tensor_copy(prob_t[0:TT, u % 2, 0:nk], ps_t[u % 2][0:TT, 0:nk])\
                        .then_inc(pt_ready.sem, 1)

                for u in range(NU + 3):
                    if u == 7:
                        dve.wait_ge(arg1_ready.sem, arg1_ready.at(b, 1))
                        nc.vector.scalar_tensor_tensor(hyp, arg, -1.0, hyp, ALU.add, ALU.mult)\
                            .then_inc(hyp_sq_ready.sem, 1)
                    if N_SDOT - 2 <= u < N_SDOT + 4:
                        i = u - (N_SDOT - 2)
                        if i == 0:
                            dve.wait_ge(hyp_scaled.sem, hyp_scaled.at(b, 1))
                        part = hyp[:, i // 2, (i % 2) * 2 * TT:(i % 2 + 1) * 2 * TT]
                        nc.vector.reciprocal(part, part)
                        if i % 2 == 1:
                            nc.vector.drain()
                    if u >= V_FROM + KC + 1 and (u - V_FROM - 1) % KC == 0 and (u - V_FROM - 1) // KC <= V_SELF:
                        v_out(b, (u - V_FROM - 1) // KC - 1)
                    if u < NU:
                        shift(u)
                    if u >= 3:
                        turned(u - 3)
                dve.wait_ge(pv_done.sem, pv_done.at(b, NU))
                inverses(b, 0)
                v_out(b, V_SELF)
                outputs(b, 0)
                dve.wait_ge(xb_ready.sem, xb_ready.at(b, 1))
                dve.wait_ge(x2_stored.sem, x2_stored.at(b, 16))
                for t in range(NT):
                    dve.wait_ge(proj_done.sem, proj_done.at(b, t + 1))
                    nc.vector.tensor_tensor(x1[:, t, :], ps_o[t][0:TT, :], x_b[:, t, :], ALU.add)\
                        .then_inc(x1_ready.sem, 1)
                nc.vector.drain()
                norm(b, x1, 1)
                for j in range(V_SELF + 1, NC):
                    v_out(b, j)
                for t in range(NT):
                    act_out(b, 1, t)
                for c in range(1, KC, 2):
                    dve.wait_ge(q2_done.sem, q2_done.at(b, c + 1))
                    for i in range(4):
                        rows = slice(HD * i, HD * (i + 1))
                        last = nc.vector.tensor_scalar(q_m[rows, 4 * c + i, :], bank[c][rows, 0:S], bq[rows, c:c + 1],
                                                       None, ALU.add)
                    last.then_inc(q2_ready[1].sem, 1)

                def masked(u):
                    t = u // H
                    dve.wait_ge(cs_done.sem, cs_done.at(b, u + 1))
                    if u >= 3:
                        dve.wait_ge(cp_ready.sem, cp_ready.at(b, u - 2))
                    nc.vector.scalar_tensor_tensor(neg_s[:, u % 3, :].rearrange("p (i n) -> p i n", i=2),
                                                   ps_s[u % 2][0:TT, :, 0:HC], 1.0 / SQRT_HD,
                                                   mask[:, t, :].rearrange("p (i n) -> p i n", i=2),
                                                   ALU.mult, ALU.mult).then_inc(cs_masked.sem, 1)

                def shifted(u):
                    t = u // H
                    dve.wait_ge(cs_masked.sem, cs_masked.at(b, u + 1))
                    dve.sem_inc(passed_dve, 1)
                    nc.vector.tensor_tensor_reduce(neg_s[:, u % 3, :], neg_s[:, u % 3, :], mask_bias[:, t, :], -1.0, 3.4e38,
                                                   ALU.add, ALU.min, neg_max[:, u:u + 1]).then_inc(cs_shifted.sem, 1)

                for u in range(NU):
                    masked(u)
                    shifted(u)
                inverses(b, 1)
                outputs(b, 1)
                dve.wait_ge(x1b_ready.sem, x1b_ready.at(b, 1))
                for t in range(NT):
                    dve.wait_ge(proj_done.sem, proj_done.at(b, NT + t + 1))
                    nc.vector.tensor_tensor(x2[:, t, :], ps_o[t][0:TT, :], x_b[:, t, :], ALU.add)\
                        .then_inc(x2_ready.sem, 1)

        @block.scalar
        def _(act):
            for dst, src in ((mask, a["mask"].rearrange("(t p) s -> p t s", p=TT)),
                             (curv, a["curv"]), (rot_cos, a["rot_cos"].rearrange("(t p) d -> p t d", p=TT)),
                             (rot_sin, a["rot_sin"].rearrange("(t p) d -> p t d", p=TT)),
                             (bk, a["bk"]), (bq, a["bq"]),
                             (proj_b, a["proj_b"].partition_broadcast(P)), (bv, a["bv"].partition_broadcast(P)),
                             (bo, a["bo"].partition_broadcast(P))):
                act.dma_start(dst[:], src).then_inc(tables_in, 16)
            act.sem_inc(x2_stored.sem, 16)
            act.wait_ge(consts, 1)
            nc.scalar.activation(root_inv_curv[:], inv_curv[:], ACT.Sqrt)

            def k_out(b, g, n):
                act.wait_ge(k_done.sem, k_done.at(b, g + 1))
                c, part = g // 2, g % 2
                nc.scalar.activation(k_t[:, c, part * HC:(part + 1) * HC], bank[n % 4][:, 0:HC], ACT.Identity,
                                     bias=bk[:, c:c + 1]).then_inc(k_ready.sem, 1)

            nc.scalar.drain().then_inc(consts, 1)
            with act.Fori(0, B) as b:
                for g in range(4):
                    k_out(b, g, g)
                for t in range(NT):
                    j = 3 * t + 2
                    act.wait_ge(qkv_done.sem, qkv_done.at(b, j + 1))
                    nc.scalar.copy(v_s[:, t, :], bank[j % 4][0:TT, :]).then_inc(vs_ready.sem, 1)
                for g in range(4, 8):
                    k_out(b, g, g + 2)

                for g in range(3 * NT):
                    t, r = g // 3, g % 3
                    if r == 1:
                        continue
                    act.wait_ge(qk_tr.sem, qk_tr.at(b, g + 1))
                    cols = slice(t * TT, (t + 1) * TT)
                    for i in range(4):
                        rows = slice(HD * i, HD * (i + 1))
                        dst = q_m[rows, i:H:4, cols] if r == 0 else q_m[rows, H + i:H + i + 1, cols]
                        n = KC if r == 0 else 1
                        last = nc.scalar.copy(dst, ps_t[g % 2][rows, 0:n * TT].rearrange("p (c n) -> p c n", n=TT))
                    if r == 2:
                        last = nc.scalar.copy(keys_t[:, KC, cols], ps_t[g % 2][:, TT:2 * TT])
                    last.then_inc(q_turned.sem, 1)
                for u in range(NU):
                    t, h = UNITS[u]
                    nk = (t + 1) * TT
                    if u == ROOT_AT:
                        act.wait_ge(hyp_sq_ready.sem, hyp_sq_ready.at(b, 1))
                        nc.scalar.activation(hyp, hyp, ACT.Sqrt).then_inc(hyp_root_ready.sem, 1)
                    if u == LN_AT:
                        act.wait_ge(hyp_sum_ready.sem, hyp_sum_ready.at(b, 1))
                        nc.scalar.activation(hyp, hyp, ACT.Ln).then_inc(hyp_ln_ready.sem, 1)
                    act.wait_ge(s_shifted.sem, s_shifted.at(b, u + 1))
                    if u >= 3:
                        act.wait_ge(p_tr.sem, p_tr.at(b, u - 2))
                    nc.scalar.activation(prob[:, u % 3, 0:nk], neg_s[:, u % 3, 0:nk], ACT.Exp,
                                         bias=neg_max[:, u:u + 1], scale=-1.0,
                                         accum_out=row_sum[:, t * H + h:t * H + h + 1]).then_inc(p_ready.sem, 1)
                for c in range(0, KC, 2):
                    act.wait_ge(q2_done.sem, q2_done.at(b, c + 1))
                    for i in range(4):
                        rows = slice(HD * i, HD * (i + 1))
                        last = nc.scalar.activation(q_m[rows, 4 * c + i, :], bank[c][rows, 0:S], ACT.Identity,
                                                    bias=bq[rows, c:c + 1])
                    last.then_inc(q2_ready[0].sem, 1)

                def cross_exp(u):
                    act.wait_ge(cs_shifted.sem, cs_shifted.at(b, u + 1))
                    if u >= 3:
                        act.wait_ge(cp_tr.sem, cp_tr.at(b, 2 * u - 4))
                    nc.scalar.activation(prob[:, u % 3, :], neg_s[:, u % 3, :], ACT.Exp, bias=neg_max[:, u:u + 1],
                                         scale=-1.0, accum_out=row_sum[:, u:u + 1]).then_inc(cp_ready.sem, 1)

                def cross_turned(u):
                    for i in range(2):
                        act.wait_ge(cp_tr.sem, cp_tr.at(b, 2 * u + i + 1))
                        if u >= 2 and i == 0:
                            act.wait_ge(cpv_done.sem, cpv_done.at(b, u - 1))
                        nc.scalar.copy(prob_t[0:CT, u % 2, i * HB:(i + 1) * HB], ps_t[i][0:CT, 0:HB])\
                            .then_inc(cpt_ready.sem, 1)

                for u in range(NU + 2):
                    if u >= 2:
                        cross_turned(u - 2)
                    if u < NU:
                        cross_exp(u)
                act.wait_ge(x2_ready.sem, x2_ready.at(b, NT))
                act.dma_start(batch_of(x2_v, b), x2[:]).then_inc(x2_stored.sem, 16)
            act.wait_ge(x2_stored.sem, 16 * (B + 1))

        @block.gpsimd
        def _(pool):
            nc.gpsimd.memset(ident[:], 0.0)
            nc.gpsimd.memset(head_rows[:], 0.0)
            nc.gpsimd.memset(q_m[:], 0.0)
            nc.gpsimd.memset(causal[:], 0.0).then_inc(pool_consts, 1)
            pool.wait_ge(pool_consts, 1)
            nc.gpsimd.affine_select(out=ident[:], in_=ident[:], compare_op=ALU.not_equal, fill=1.0, base=0,
                                    pattern=[[-1, P]], channel_multiplier=1).then_inc(pool_consts, 1)
            nc.gpsimd.affine_select(out=head_rows[:].rearrange("r k (g d) -> r k g d", d=HD),
                                    in_=head_rows[:].rearrange("r k (g d) -> r k g d", d=HD),
                                    compare_op=ALU.not_equal, fill=1.0, base=0,
                                    pattern=[[-4, NT * KC], [-1, 4], [0, HD]], channel_multiplier=1)
            nc.gpsimd.affine_select(out=causal[:, 0:TT], in_=causal[:, 0:TT], compare_op=ALU.is_ge, fill=NEG, base=0,
                                    pattern=[[-1, TT]], channel_multiplier=1)
            nc.gpsimd.affine_select(out=causal[:, TT:], in_=causal[:, TT:], compare_op=ALU.is_ge, fill=NEG, base=TT,
                                    pattern=[[-1, S]], channel_multiplier=1).then_inc(pool_consts, 1)
            pool.wait_ge(consts, 2)
            with pool.Fori(0, B) as b:
                def root(k):
                    pool.wait_ge(var_ready.sem, var_ready.at(b, k + 1))
                    nc.gpsimd.tensor_tensor(rstd[:], var_eps[:], minus_half[:], ALU.pow).then_inc(rstd_ready.sem, 1)

                root(0)
                nc.gpsimd.tensor_tensor(x_b[:], x_in[:], spread(proj_b[0:TT, :], 1, NT), ALU.add)\
                    .then_inc(xb_ready.sem, 1)
                for r in range(2 * NT):
                    pool.wait_ge(rot_parts.sem, rot_parts.at(b, r + 1))
                    nc.gpsimd.tensor_tensor(qk[:, r, 0:D], rot_a[:, r % 2, :], rot_b[:, r % 2, :], ALU.add)\
                        .then_inc(rot_ready.sem, 1)
                    pool.wait_ge(rot_ready.sem, rot_ready.at(b, r + 1))
                    if r >= 2:
                        pool.wait_ge(sq_used.sem, sq_used.at(b, r - 1))
                    heads = qk[:, r, N_SDPA * HD:D]
                    nc.gpsimd.tensor_tensor(squares[:, r % 2, :], heads, heads, ALU.mult).then_inc(sq_ready.sem, 1)
                pool.wait_ge(sums_ready.sem, sums_ready.at(b, 1))
                nc.gpsimd.tensor_tensor(norms[:].rearrange("p r h -> p (r h)"), sums[:].rearrange("p r h -> p (r h)"),
                                        half[:], ALU.pow).then_inc(norms_ready.sem, 1)
                pool.wait_ge(arg_ready.sem, arg_ready.at(b, N_HYP * NT))
                pool.sem_inc(passed_pool, 1)
                nc.gpsimd.tensor_scalar(hyp, arg, 1.0, None, ALU.add).then_inc(arg1_ready.sem, 1)
                pool.wait_ge(hyp_root_ready.sem, hyp_root_ready.at(b, 1))
                nc.gpsimd.tensor_tensor(hyp, hyp, arg, ALU.add).then_inc(hyp_sum_ready.sem, 1)
                pool.wait_ge(hyp_ln_ready.sem, hyp_ln_ready.at(b, 1))
                pool.sem_inc(passed_pool, 1)
                for hh in range(N_HYP):
                    part = hyp[:, :, hh * TT:(hh + 1) * TT]
                    last = nc.gpsimd.tensor_scalar(part, part, root_inv_curv[0:TT, hh:hh + 1], 1e-6, ALU.mult, ALU.add)
                last.then_inc(hyp_scaled.sem, 1)
                root(1)
                nc.gpsimd.tensor_tensor(x_b[:], x1[:], spread(bo[0:TT, :], 1, NT), ALU.add)\
                    .then_inc(x1b_ready.sem, 1)


HF = 8
KD = 128
NK = 128
TOP = 8
NF = 2 * HF
TOK = B * S
NTF = TOK // P
QC = 4
QN = TOK // QC
TPB = 4
BN_EPS = 1e-5
PICK = HF * TOP
GELU_C = (2.0 / 3.141592653589793) ** 0.5


def in_turn(eng, first, second):
    first(0, 0)
    with eng.Fori(0, NF // 2 - 1) as i:
        first(2 * i + 1, 1)
        second(2 * i, 0)
        first(2 * i + 2, 0)
        second(2 * i + 1, 1)
    first(NF - 1, 1)
    second(NF - 2, 0)
    second(NF - 1, 1)


def build_queries(nc, a, x2_dram, xn_all, top_val, top_idx, ident):
    with ExitStack() as ctx:
        def sb(name, shape, dt=F32):
            return ctx.enter_context(nc.sbuf_tensor("q_" + name, shape, dt))

        def psum(name, shape):
            return ctx.enter_context(nc.psum_tensor("q_" + name, shape, F32))

        def sem(name):
            return ctx.enter_context(nc.semaphore("q_" + name))

        x_in = sb("x_in", [P, 2, D])
        xn = sb("xn", [P, 2, D])
        stats = sb("stats", [P, QC, 6])
        mean_var = sb("mean_var", [P, 2])
        var_eps = sb("var_eps", [P, 1])
        rstd = sb("rstd", [P, 1])
        minus_half = sb("minus_half", [P, 1])
        xn_t = sb("xn_t", [P, KC, TOK])
        w_q = sb("w_q", [P, 2, KC, KD])
        keys = sb("keys", [P, 2, NK])
        gamma = sb("gamma", [P, NF])
        beta = sb("beta", [P, NF])
        scale = sb("scale", [P, 2])
        shift = sb("shift", [P, 2])
        q_t = sb("q_t", [P, 2, TOK])
        sims = sb("sims", [P, 2, TOK])
        best = sb("best", [P, 2, NTF, TOP])
        best_at = sb("best_at", [P, 2, NTF, TOP], U32)

        ps_q = [psum(f"ps_q{i}", [P, 512]) for i in range(QC)]
        ps_m = [psum(f"ps_m{i}", [P, 512]) for i in range(4)]
        n_banks = -(-NTF // TPB)

        small_in = sem("small_in")
        x_loaded = [sem(f"x_loaded{s}") for s in range(2)]
        normed = sem("normed")
        var_ready = sem("var_ready")
        rstd_ready = sem("rstd_ready")
        copied = sem("copied")
        turned = sem("turned")
        turned_out = sem("turned_out")
        half_ready = sem("half_ready")
        w_loaded = [sem(f"w_loaded{s}") for s in range(2)]
        q_done = sem("q_done")
        affine_ready = sem("affine_ready")
        bn_var = sem("bn_var")
        bn_rstd = sem("bn_rstd")
        q_ready = sem("q_ready")
        sims_done = sem("sims_done")
        sims_ready = sem("sims_ready")
        best_done = sem("best_done")
        best_kept = sem("best_kept")
        passed = sem("passed")

        x2_v = x2_dram.rearrange("(n p) d -> n p d", p=P)

        def tile_of(view, i):
            return view[bass.ds(i, 1)].rearrange("o p d -> (o p) d")

        block = ctx.enter_context(nc.Block())

        @block.sync
        def _(sp):
            sp.dma_start(gamma[:], a["gamma"]).then_inc(small_in, 16)
            sp.dma_start(beta[:], a["beta"]).then_inc(small_in, 16)
            for s in range(2):
                sp.dma_start(x_in[:, s, :], x2_v[s]).then_inc(x_loaded[s], 16)
            w_v = a["ffn_wq"].rearrange("(c p) (f n) -> f p c n", p=P, n=KD)
            k_v = a["keys_t"].rearrange("p (f n) -> f p n", n=NK)

            def block_in(f, s):
                src = w_v[bass.ds(f, 1)].rearrange("o p c n -> (o p) c n")
                sp.dma_start(w_q[:, s], src).then_inc(w_loaded[s], 16)
                src = k_v[bass.ds(f, 1)].rearrange("o p n -> (o p) n")
                sp.dma_start(keys[:, s], src).then_inc(w_loaded[s], 16)

            for s in range(2):
                block_in(s, s)
            with sp.Fori(0, NTF // 2 - 1) as i:
                for s in range(2):
                    sp.wait_ge(normed, 2 * i + s + 1)
                    sp.dma_start(x_in[:, s, :], tile_of(x2_v, 2 * i + 2 + s)).then_inc(x_loaded[s], 16)
            with sp.Fori(0, NF // 2 - 1) as i:
                for s in range(2):
                    sp.wait_ge(sims_done, 2 * i + s + 2)
                    block_in(2 * i + 2 + s, s)

        @block.gpsimd
        def _(pool):
            nc.gpsimd.memset(minus_half[:], -0.5).then_inc(half_ready, 1)
            nc.gpsimd.memset(top_val[:, :, NTF, :], 0.0)
            nc.gpsimd.memset(top_idx[:, :, NTF, :], 0.0)
            pool.sem_inc(copied, 2)
            pool.sem_inc(best_kept, 2)
            pool.wait_ge(half_ready, 1)
            with pool.Fori(0, NTF // 2) as i:
                for s in range(2):
                    pool.wait_ge(var_ready, 2 * i + s + 1)
                    nc.gpsimd.tensor_tensor(rstd[:], var_eps[:], minus_half[:], ALU.pow).then_inc(rstd_ready, 1)
                    pool.wait_ge(normed, 2 * i + s + 1)
                    nc.gpsimd.tensor_copy(xn_all[:, bass.ds(2 * i + s, 1), :].rearrange("p o d -> p (o d)"),
                                          xn[:, s, :]).then_inc(copied, 1)

            def first(f, s):
                pool.wait_ge(bn_var, f + 1)
                nc.gpsimd.tensor_tensor(rstd[:], var_eps[:], minus_half[:], ALU.pow).then_inc(bn_rstd, 1)

            def second(f, s):
                pool.wait_ge(best_done, f + 3)
                for dst, src in ((top_val, best), (top_idx, best_at)):
                    last = nc.gpsimd.tensor_copy(dst[:, bass.ds(f, 1), 0:NTF, :].rearrange("p o n k -> p (o n) k"),
                                                 src[:, s])
                last.then_inc(best_kept, 1)

            in_turn(pool, first, second)

        @block.tensor
        def _(pe):
            pe.sem_inc(turned, 2)
            pe.sem_inc(sims_done, 1)
            with pe.Fori(0, NTF // 2) as i:
                for s in range(2):
                    pe.wait_ge(normed, 2 * i + s + 1)
                    pe.wait_ge(turned_out, 2 * i + s + 1)
                    for c in range(KC):
                        mm = nc.tensor.transpose(ps_q[s][:, c * P:(c + 1) * P], xn[:, s, c * P:(c + 1) * P], ident[:])
                    mm.then_inc(turned, 1)

            def first(f, s):
                half = f // 2 if isinstance(f, int) else None
                pe.wait_ge(w_loaded[s], 32 * (half + 1) if half is not None else (f - s) * 16 + 32)
                for c in range(QC):
                    if not isinstance(f, int) or f > 0:
                        pe.wait_ge(q_ready, QC * f - QC + c + 1)
                    for kc in range(KC):
                        mm = nc.tensor.matmul(ps_q[c][:, 0:QN], w_q[:, s, kc, :], xn_t[:, kc, c * QN:(c + 1) * QN],
                                              start=(kc == 0), stop=(kc == KC - 1))
                    mm.then_inc(q_done, 1)

            def second(f, s):
                pe.wait_ge(q_ready, QC * f + QC)
                for i in range(NTF):
                    if i % TPB == 0:
                        pe.wait_ge(sims_ready, n_banks * f + i // TPB + 1)
                    mm = nc.tensor.matmul(ps_m[i // TPB][:, (i % TPB) * NK:(i % TPB + 1) * NK],
                                          q_t[:, s, i * P:(i + 1) * P], keys[:, s, :], start=True, stop=True)
                mm.then_inc(sims_done, 1)

            pe.wait_ge(turned_out, NTF + 2)
            in_turn(pe, first, second)

        @block.vector
        def _(dve):
            with dve.Fori(0, NTF // 2) as i:
                for s in range(2):
                    dve.wait_ge(x_loaded[s], 16 * i + 16)
                    nc.vector.bn_stats(stats[:, 0, :], x_in[:, s, :])
                    nc.vector.drain()
                    nc.vector.bn_aggr(mean_var[:], stats[:, 0, :])
                    nc.vector.drain()
                    nc.vector.tensor_scalar(var_eps[:], mean_var[:, 1:2], LN_EPS, None, ALU.add).then_inc(var_ready, 1)
                    dve.wait_ge(copied, 2 * i + s + 1)
                    dve.wait_ge(turned, 2 * i + s + 1)
                    dve.wait_ge(rstd_ready, 2 * i + s + 1)
                    nc.vector.tensor_scalar(xn[:, s, :], x_in[:, s, :], mean_var[:, 0:1], rstd[:], ALU.subtract,
                                            ALU.mult).then_inc(normed, 1)

            def first(f, s):
                for c in range(QC):
                    dve.wait_ge(q_done, QC * f + c + 1)
                    nc.vector.bn_stats(stats[:, c, :], ps_q[c][:, 0:QN])
                nc.vector.drain()
                nc.vector.bn_aggr(mean_var[:], stats[:].rearrange("p c n -> p (c n)"))
                nc.vector.drain()
                nc.vector.tensor_scalar(var_eps[:], mean_var[:, 1:2], BN_EPS, None, ALU.add).then_inc(bn_var, 1)
                dve.wait_ge(bn_rstd, f + 1)
                nc.vector.tensor_tensor(scale[:, s:s + 1], rstd[:], gamma[:, bass.ds(f, 1)], ALU.mult)
                nc.vector.drain()
                nc.vector.tensor_tensor(shift[:, s:s + 1], mean_var[:, 0:1], scale[:, s:s + 1], ALU.mult)
                nc.vector.drain()
                nc.vector.tensor_tensor(shift[:, s:s + 1], beta[:, bass.ds(f, 1)], shift[:, s:s + 1], ALU.subtract)\
                    .then_inc(affine_ready, 1)

            def second(f, s):
                dve.wait_ge(best_kept, f + 1)
                dve.wait_ge(sims_ready, n_banks * f + 2 * n_banks)
                dve.sem_inc(passed, 1)
                for i in range(NTF):
                    nc.vector.max(best[:, s, i, :], sims[:, s, i * P:(i + 1) * P])
                nc.vector.drain()
                for i in range(NTF):
                    last = nc.vector.max_index(best_at[:, s, i, :], best[:, s, i, :], sims[:, s, i * P:(i + 1) * P])
                last.then_inc(best_done, 1)

            dve.wait_ge(small_in, 32)
            dve.sem_inc(best_done, 2)
            in_turn(dve, first, second)

        @block.scalar
        def _(act):
            act.sem_inc(turned_out, 2)
            act.sem_inc(sims_ready, n_banks)
            with act.Fori(0, NTF // 2) as i:
                for s in range(2):
                    act.wait_ge(turned, 2 * i + s + 1 + 2)
                    nc.scalar.copy(xn_t[:, :, bass.ds((2 * i + s) * P, P)],
                                   ps_q[s][:].rearrange("p (c n) -> p c n", c=KC)).then_inc(turned_out, 1)

            def first(f, s):
                act.wait_ge(affine_ready, f + 1)
                if not isinstance(f, int) or f > 0:
                    act.wait_ge(sims_done, f)
                for c in range(QC):
                    nc.scalar.activation(q_t[:, s, c * QN:(c + 1) * QN], ps_q[c][:, 0:QN], ACT.Identity,
                                         bias=shift[:, s:s + 1], scale=scale[:, s:s + 1]).then_inc(q_ready, 1)

            def second(f, s):
                act.wait_ge(sims_done, f + 2)
                act.wait_ge(best_done, f + 1)
                for k in range(n_banks):
                    n = min(TPB, NTF - k * TPB) * NK
                    nc.scalar.copy(sims[:, s, k * TPB * NK:k * TPB * NK + n], ps_m[k][:, 0:n])\
                        .then_inc(sims_ready, 1)

            in_turn(act, first, second)


def build_experts(nc, a, x2_dram, out, xn_all, top_val, top_idx, ident):
    with ExitStack() as ctx:
        def sb(name, shape, dt=F32):
            return ctx.enter_context(nc.sbuf_tensor("e_" + name, shape, dt))

        def psum(name, shape):
            return ctx.enter_context(nc.psum_tensor("e_" + name, shape, F32))

        def sem(name):
            return ctx.enter_context(nc.semaphore("e_" + name))

        HALF = HF // 2
        rows = sb("rows", [P, HALF, TOP, 2 * D])
        idx_all = sb("idx_all", [P, NTF + 1, PICK], U32)
        gate_all = sb("gate_all", [P, NTF + 1, PICK])
        idx = sb("idx", [P, 2, PICK // 2], U32)
        x_t = sb("x_t", [P, D])
        product = sb("product", [P, TOP // 2, D])
        hidden = sb("hidden", [P, 2, TOP])
        cubic = sb("cubic", [P, 2, TOP])
        tanh = sb("tanh", [P, 2, TOP])
        weight = sb("weight", [P, 2, TOP])
        diag = sb("diag", [P, 2, TOP, P])
        pair = sb("pair", [P, HF, TOP, TOP])
        match = pair
        best = sb("best", [P, HF, TOP])
        at = sb("at", [P, HF, TOP], U32)
        at_x = sb("at_x", [P, PICK], U32)
        at_y = sb("at_y", [P, PICK], U32)
        at_f = sb("at_f", [P, 2, PICK])
        chosen = sb("chosen", [P, 2, PICK])
        eight = sb("eight", [P, TOP])
        soft = sb("soft", [P, HF, TOP])
        soft_sum = sb("soft_sum", [P, HF])
        x2_t = sb("x2_t", [P, D])
        out_t = sb("out_t", [P, D])
        ps_out = psum("ps_out", [P, 512])

        rows_in = [sem(f"rows_in{g}") for g in range(HALF)]
        iota_ready = sem("iota_ready")
        idx_ready = sem("idx_ready")
        idx_here = sem("idx_here")
        soft_in = sem("soft_in")
        soft_out = sem("soft_out")
        cubic_ready = sem("cubic_ready")
        tanh_ready = sem("tanh_ready")
        weight_ready = sem("weight_ready")
        diag_ready = sem("diag_ready")
        rows_used = sem("rows_used")
        x2_loaded = sem("x2_loaded")
        out_ready = sem("out_ready")
        out_stored = sem("out_stored")
        passed = sem("passed")

        x2_v = x2_dram.rearrange("(n p) d -> n p d", p=P)
        out_v = out.rearrange("b s d -> (b s) d").rearrange("(n p) d -> n p d", p=P)
        table = a["experts"]

        def tile_of(view, i):
            return view[bass.ds(i, 1)].rearrange("o p d -> (o p) d")

        block = ctx.enter_context(nc.Block())

        @block.sync
        def _(sp):
            sp.dma_start(x2_t[:], x2_v[0]).then_inc(x2_loaded, 16)
            with sp.Fori(0, NTF - 1) as t:
                sp.wait_ge(out_ready, t + 2)
                sp.dma_start(x2_t[:], tile_of(x2_v, t + 1)).then_inc(x2_loaded, 16)
                sp.dma_start(tile_of(out_v, t), out_t[:]).then_inc(out_stored, 16)
            sp.wait_ge(out_ready, NTF + 1)
            sp.dma_start(out_v[NTF - 1], out_t[:]).then_inc(out_stored, 16)
            sp.wait_ge(out_stored, 16 * (NTF + 1))

        @block.gpsimd
        def _(pool):
            nc.gpsimd.iota(eight[:], [[1, TOP]], channel_multiplier=0, allow_small_or_imprecise_dtypes=True)\
                .then_inc(iota_ready, 1)
            with pool.Fori(0, NTF) as t:
                for half in range(2):
                    pool.wait_ge(idx_ready, 2 * t + half + 1)
                    n = PICK // 2
                    nc.gpsimd.tensor_copy(idx[:, half, :],
                                          idx_all[:, bass.ds(t, 1), half * n:(half + 1) * n]
                                          .rearrange("p o k -> p (o k)")).then_inc(idx_here, 1)
                    pool.wait_ge(idx_here, 2 * t + half + 1)
                    for g in range(HALF):
                        pool.wait_ge(rows_used, HF * t + HALF * half + g + 1)
                        pool.sem_inc(passed, 1)
                        for k in range(TOP):
                            pool.indirect_dma_start(
                                rows[:, g, k, :], None, table[:, :],
                                bass.IndirectOffsetOnAxis(ap=idx[:, half, g * TOP + k:g * TOP + k + 1], axis=0))\
                                .then_inc(rows_in[g], 16)

        @block.vector
        def _(dve):
            def choose(t):
                def of(top, half):
                    return top[:, half * HF:(half + 1) * HF, bass.ds(t, 1), :].rearrange("p h o k -> p h (o k)")

                nc.vector.tensor_tensor(pair[:], spread(of(top_val, 0), 3, TOP), spread(of(top_val, 1), 2, TOP), ALU.add)
                nc.vector.drain()
                for h in range(HF):
                    nc.vector.max(best[:, h, :], pair[:, h].rearrange("p x y -> p (x y)"))
                nc.vector.drain()
                for h in range(HF):
                    nc.vector.max_index(at[:, h, :], best[:, h, :], pair[:, h].rearrange("p x y -> p (x y)"))
                nc.vector.tensor_tensor(soft[:], best[:], spread(best[:, :, 0], 2, TOP), ALU.subtract)\
                    .then_inc(soft_in, 1)
                nc.vector.drain()
                flat = at[:].rearrange("p h k -> p (h k)")
                nc.vector.tensor_scalar(at_x[:], flat, 3, None, ALU.logical_shift_right)
                nc.vector.tensor_scalar(at_y[:], flat, TOP - 1, None, ALU.bitwise_and)
                nc.vector.drain()
                nc.vector.tensor_copy(at_f[:, 0, :], at_x[:])
                nc.vector.tensor_copy(at_f[:, 1, :], at_y[:])
                for half in range(2):
                    nc.vector.drain()
                    nc.vector.tensor_tensor(match[:].rearrange("p h k j -> p (h k) j"), spread(at_f[:, half, :], 2, TOP),
                                            spread(eight[:], 1, PICK), ALU.is_equal)
                    nc.vector.drain()
                    nc.vector.tensor_tensor(match[:], match[:], spread(of(top_idx, half), 2, TOP), ALU.mult)
                    nc.vector.drain()
                    nc.vector.tensor_reduce(chosen[:, half, :], match[:].rearrange("p h k j -> p (h k) j"), AX_X,
                                            ALU.add)
                nc.vector.drain()
                here = idx_all[:, bass.ds(t, 1), :].rearrange("p o k -> p (o k)")
                nc.vector.scalar_tensor_tensor(here, chosen[:, 0, :], float(NK), chosen[:, 1, :], ALU.mult, ALU.add)\
                    .then_inc(idx_ready, 2)
                dve.wait_ge(soft_out, t + 1)
                nc.vector.tensor_reduce(soft_sum[:], soft[:], AX_X, ALU.add)
                nc.vector.drain()
                nc.vector.reciprocal(soft_sum[:], soft_sum[:])
                nc.vector.drain()
                nc.vector.tensor_tensor(gate_all[:, bass.ds(t, 1), :].rearrange("p o (h k) -> p (o h) k", k=TOP),
                                        soft[:], spread(soft_sum[:], 2, TOP), ALU.mult)
                nc.vector.drain()

            def weights(t, n):
                s = n % 2
                dve.wait_ge(tanh_ready, HF * t + n + 1)
                nc.vector.scalar_tensor_tensor(tanh[:, s, :], tanh[:, s, :], 1.0, hidden[:, s, :], ALU.add, ALU.mult)
                nc.vector.drain()
                nc.vector.scalar_tensor_tensor(weight[:, s, :], tanh[:, s, :], 0.5,
                                               gate_all[:, bass.ds(t, 1), n * TOP:(n + 1) * TOP]
                                               .rearrange("p o k -> p (o k)"), ALU.mult, ALU.mult)\
                    .then_inc(weight_ready, 1)

            dve.wait_ge(iota_ready, 1)
            choose(0)
            with dve.Fori(0, NTF) as t:
                nc.vector.tensor_copy(x_t[:], xn_all[:, bass.ds(t, 1), :].rearrange("p o d -> p (o d)"))
                nc.vector.drain()
                for n in range(HF):
                    g, s = n % HALF, n % 2
                    dve.wait_ge(rows_in[g], (2 * t + n // HALF) * (16 * TOP) + 16 * TOP)
                    for k in range(TOP):
                        if k == TOP // 2:
                            nc.vector.drain()
                        nc.vector.tensor_tensor_reduce(product[:, k % (TOP // 2), :], rows[:, g, k, 0:D], x_t[:], 1.0, 0.0, ALU.mult,
                                                       ALU.add, hidden[:, s, k:k + 1])
                        if k == 1 and n >= 1:
                            weights(t, n - 1)
                    nc.vector.drain()
                    nc.vector.scalar_tensor_tensor(cubic[:, s, :], hidden[:, s, :], 0.044715, hidden[:, s, :],
                                                   ALU.mult, ALU.mult)
                    nc.vector.drain()
                    nc.vector.scalar_tensor_tensor(cubic[:, s, :], cubic[:, s, :], 1.0, hidden[:, s, :], ALU.add,
                                                   ALU.mult).then_inc(cubic_ready, 1)
                    if n == 2:
                        choose(t + 1)
                weights(t, HF - 1)
                dve.wait_ge(rows_used, HF * t + HF + HALF)
                dve.wait_ge(x2_loaded, 16 * t + 16)
                dve.wait_ge(out_stored, 16 * t + 16)
                nc.vector.tensor_tensor(out_t[:], ps_out[:], x2_t[:], ALU.add).then_inc(out_ready, 1)

        @block.scalar
        def _(act):
            act.sem_inc(out_stored, 16)

            def soften(t):
                act.wait_ge(soft_in, t + 1)
                nc.scalar.activation(soft[:], soft[:], ACT.Exp).then_inc(soft_out, 1)

            soften(0)
            with act.Fori(0, NTF) as t:
                for n in range(HF):
                    s = n % 2
                    act.wait_ge(cubic_ready, HF * t + n + 1)
                    nc.scalar.activation(tanh[:, s, :], cubic[:, s, :], ACT.Tanh, scale=GELU_C)\
                        .then_inc(tanh_ready, 1)
                    if n == 2:
                        soften(t + 1)
                    act.wait_ge(weight_ready, HF * t + n + 1)
                    act.wait_ge(rows_used, HF * t + n + HALF - 1)
                    for k in range(TOP):
                        last = nc.scalar.activation(diag[:, s, k, :], ident[:], ACT.Copy, scale=weight[:, s, k:k + 1])
                        last.then_inc(diag_ready, 1)

        @block.tensor
        def _(pe):
            pe.sem_inc(rows_used, HALF)
            pe.sem_inc(out_ready, 1)
            with pe.Fori(0, NTF) as t:
                pe.wait_ge(out_ready, t + 1)
                pe.sem_inc(passed, 1)
                for n in range(HF):
                    for k in range(TOP):
                        pe.wait_ge(diag_ready, PICK * t + n * TOP + k + 1)
                        mm = nc.tensor.matmul(ps_out[:], diag[:, n % 2, k, :], rows[:, n % HALF, k, D:],
                                              start=(n + k == 0), stop=(n * TOP + k == PICK - 1))
                    mm.then_inc(rows_used, 1)


def build(nc, a, out):
    x2_dram = nc.dram_tensor("x2_dram", [TOK, D], F32, kind="Internal").ap()
    build_attention(nc, a, x2_dram)
    with ExitStack() as ctx:
        def sb(name, shape):
            return ctx.enter_context(nc.sbuf_tensor(name, shape, F32))

        xn_all = sb("xn_all", [P, NTF, D])
        top_val = sb("top_val", [P, NF, NTF + 1, TOP])
        top_idx = sb("top_idx", [P, NF, NTF + 1, TOP])
        ident = sb("ident_f", [P, P])
        with ExitStack() as setup:
            ready = setup.enter_context(nc.semaphore("ident_ready"))
            block = setup.enter_context(nc.Block())

            @block.gpsimd
            def _(pool):
                nc.gpsimd.memset(ident[:], 0.0).then_inc(ready, 1)
                pool.wait_ge(ready, 1)
                nc.gpsimd.affine_select(out=ident[:], in_=ident[:], compare_op=ALU.not_equal, fill=1.0, base=0,
                                        pattern=[[-1, P]], channel_multiplier=1)

        build_queries(nc, a, x2_dram, xn_all, top_val, top_idx, ident)
        build_experts(nc, a, x2_dram, out, xn_all, top_val, top_idx, ident)


def kernel(**inputs):
    import numpy as np
    import concourse.bacc as bacc
    from concourse import mybir as mb
    from concourse.bass_utils import run_bass_kernel_spmd as run

    rows = np.concatenate([np.arange(h * HD, (h + 1) * HD) for h in HEADS])
    qkv = inputs["L0_attn_qkv_w"].reshape(3, D, D)[:, rows, :].reshape(3 * D, D)
    half = HD // 2
    freqs = np.outer(np.arange(S, dtype=np.float32),
                     1.0 / 10000.0 ** (np.arange(0, HD, 2, dtype=np.float32) / HD)).astype(np.float32)
    cos, sin = np.cos(freqs).astype(np.float32), np.sin(freqs).astype(np.float32)
    arrays = {
        "x": inputs["x"],
        "ctx_t": inputs["ctx_1024"].transpose(0, 2, 1),
        "mask": inputs["mask_1x1xSxS2_fk0"].reshape(S, SC),
        "w_qkv_t": qkv.T,
        "w_proj_t": inputs["L0_attn_proj_w"][:, rows].T,
        "proj_b": inputs["L0_attn_proj_b"],
        "curv": np.broadcast_to(inputs["L0_attn_curvature"].reshape(1, N_HYP), (P, N_HYP)),
        "rot_cos": np.concatenate([cos, cos], axis=1),
        "rot_sin": np.concatenate([sin, -sin], axis=1),
        "wq": inputs["L0_xattn_Wq"], "wk": inputs["L0_xattn_Wk"], "wv": inputs["L0_xattn_Wv"],
        "wo": inputs["L0_xattn_Wo"], "bq": inputs["L0_xattn_bq"].reshape(KC, P).T, "bk": inputs["L0_xattn_bk"].reshape(KC, P).T,
        "bv": inputs["L0_xattn_bv"], "bo": inputs["L0_xattn_bo"],
        "ffn_wq": inputs["L0_ffn_w_q"],
        "gamma": inputs["L0_ffn_bn_gamma"].reshape(NF, KD).T,
        "beta": inputs["L0_ffn_bn_beta"].reshape(NF, KD).T,
        "keys_t": inputs["L0_ffn_keys"].transpose(3, 2, 0, 1).reshape(KD, NF * NK),
        "experts": np.concatenate([inputs["L0_ffn_down_embed"], inputs["L0_ffn_up_embed"]], axis=1),
    }
    arrays = {k: np.ascontiguousarray(v) for k, v in arrays.items()}
    nc = bacc.Bacc("TRN2", target_bir_lowering=False, num_devices=1)
    aps = {k: nc.dram_tensor("in_" + k, v.shape, mb.dt.from_np(v.dtype), kind="ExternalInput").ap() for k, v in arrays.items()}
    out = nc.dram_tensor("out_0", (B, S, D), mb.dt.float32, kind="ExternalOutput").ap()
    build(nc, aps, out)
    return run(nc, [{"in_" + k: v for k, v in arrays.items()}], core_ids=[0]).results[0]["out_0"]
```

```python
from contextlib import ExitStack

import concourse.bass as bass
from concourse import mybir

F32 = mybir.dt.float32
U32 = mybir.dt.uint32
ALU = mybir.AluOpType
ACT = mybir.ActivationFunctionType
AX_X = mybir.AxisListType.X

B, S, D = 8, 224, 512
SC = 750
H, HD = 16, 32
N_SDPA, N_HYP, N_COS = 6, 4, 6
N_DOT = N_SDPA + N_COS
HEADS = (*range(N_SDPA), *range(N_SDPA + N_HYP, H), *range(N_SDPA, N_SDPA + N_HYP))
P = 128
KC = D // P
TT = 112
NT = S // TT
CT, NC = 125, SC // 125
HC = SC // 2
HB = 3 * TT
NU = NT * H
HYW = TT + S
LN_EPS = 1e-5
NEG = -3.0e38

SQRT_HD = float(HD) ** 0.5


def spread(ap, axis, n):
    ap = ap.unsqueeze(axis)
    shape = list(ap.shape)
    shape[axis] = n
    return ap.to_broadcast(shape)


class Steps:

    def __init__(self, sem, per):
        self.sem, self.per = sem, per

    def at(self, b, n):
        return b * self.per + n


def self_units():
    return ([(t, h) for t in range(NT) for h in range(N_DOT)]
            + [(t, h) for t in range(NT) for h in range(N_DOT, H)])


UNITS = self_units()
N_SDOT = NT * N_DOT
V_SELF, V_FROM = 4, 5
ROOT_AT, LN_AT = 8, 13
RECIP_AT = 15


def build_attention(nc, a, x2_dram):
    with ExitStack() as ctx:
        def sb(name, shape, dt=F32):
            return ctx.enter_context(nc.sbuf_tensor(name, shape, dt))

        def psum(name, shape):
            return ctx.enter_context(nc.psum_tensor(name, shape, F32))

        def sem(name):
            return ctx.enter_context(nc.semaphore(name))

        def steps(name, per):
            return Steps(sem(name), per)

        w_qkv = sb("w_qkv", [P, KC, 3 * D])
        w_proj = sb("w_proj", [P, KC, D])
        w_q = sb("w_q", [P, KC, D])
        w_k = sb("w_k", [P, KC, D])
        w_v = sb("w_v", [P, KC, D])
        w_o = sb("w_o", [P, KC, D])
        proj_b = sb("proj_b", [P, D])
        bv = sb("bv", [P, D])
        bo = sb("bo", [P, D])
        bq = sb("bq", [P, KC])
        bk = sb("bk", [P, KC])
        rot_cos = sb("rot_cos", [TT, NT, HD])
        rot_sin = sb("rot_sin", [TT, NT, HD])
        curv = sb("curv", [P, N_HYP])
        mask = sb("mask", [TT, NT, SC])
        mask_bias = sb("mask_bias", [TT, NT, SC])
        ident = sb("ident", [P, P])
        causal = sb("causal", [TT, HYW])
        minus_half = sb("minus_half", [TT, NT])
        neg_curv = sb("neg_curv", [P, N_HYP])
        inv_curv = sb("inv_curv", [P, N_HYP])
        root_inv_curv = sb("root_inv_curv", [P, N_HYP])
        norm_add = sb("norm_add", [TT, N_COS + N_HYP])
        factor = sb("factor", [TT, 2 * NT, H])

        x_in = sb("x_in", [TT, NT, D])
        ctx_t = sb("ctx_t", [P, KC, SC])
        k_t = sb("k_t", [P, KC, SC])
        v_c = sb("v_c", [CT, NC, D])
        x_b = sb("x_b", [TT, NT, D])
        x_n = sb("x_n", [TT, NT, D])
        act_t = sb("act_t", [P, KC, S])
        stats = sb("stats", [TT, NT, 6])
        mean_var = sb("mean_var", [TT, NT, 2])
        var_eps = sb("var_eps", [TT, NT])
        rstd = sb("rstd", [TT, NT])
        qk = sb("qk", [TT, 2 * NT, D + P])
        sums = sb("sums", [TT, 2 * NT, N_COS + N_HYP])
        norms = sb("norms", [TT, 2 * NT, N_COS + N_HYP])
        v_s = sb("v_s", [TT, NT, D])
        keys_t = sb("keys_t", [P, KC + 1, S])
        q_m = sb("q_m", [P, H + N_HYP, S])
        neg_s = sb("neg_s", [TT, 3, SC])
        neg_max = sb("neg_max", [TT, NU])
        prob = sb("prob", [TT, 3, SC])
        room = prob[:].rearrange("p i n -> p (i n)")
        rot_a = room[:, 0:2 * D].rearrange("p (i n) -> p i n", i=2)
        rot_b = room[:, 2 * D:4 * D].rearrange("p (i n) -> p i n", i=2)
        squares = neg_s[:, 0:2, 0:(N_COS + N_HYP) * HD]
        arg = neg_s[:, :, S:S + N_HYP * TT]
        hyp = qk[:, 0:3, 0:N_HYP * TT]
        prob_t = sb("prob_t", [P, 2, 2 * HB])
        row_sum = sb("row_sum", [TT, NU])
        inv_sum = sb("inv_sum", [NU, TT])
        head_rows = sb("head_rows", [NU, NT * KC, P])
        x1 = sb("x1", [TT, NT, D])
        x2 = x1
        inv_spread = keys_t[:].rearrange("p c s -> p (c s)")[:, 0:NT * KC * TT].rearrange("p (t n) -> p t n", t=NT)

        ps_s = [psum(f"ps_s{i}", [P, 2, 512]) for i in range(2)]
        bank = [ps_s[0][:, 0, :], ps_s[0][:, 1, :], ps_s[1][:, 0, :], ps_s[1][:, 1, :]]
        ps_t = [psum(f"ps_t{i}", [P, 512]) for i in range(2)]
        ps_o = [psum(f"ps_o{i}", [P, 512]) for i in range(2)]

        def hyp_part(blocks, t, hh):
            return blocks[:, t:2 * t + 1, hh * TT:(hh + 1) * TT]

        def by_tile(ap):
            return ap.rearrange("p (k n) -> p k n", n=TT)

        passed_dve = sem("passed_dve")
        passed_pool = sem("passed_pool")
        w_k_in = sem("w_k_in")
        w_qkv_in = sem("w_qkv_in")
        weights_in = sem("weights_in")
        tables_in = sem("tables_in")
        x_loaded = steps("x_loaded", 16)
        ctx_loaded = steps("ctx_loaded", 16)
        consts = sem("consts")
        pool_consts = sem("pool_consts")
        var_ready = steps("var_ready", 2)
        rstd_ready = steps("rstd_ready", 2)
        xn_ready = steps("xn_ready", 2 * NT)
        xb_ready = steps("xb_ready", 1)
        act_tr = steps("act_tr", 2 * NT)
        act_ready = steps("act_ready", 4 * NT)
        k_done = steps("k_done", 2 * KC)
        k_ready = steps("k_ready", 2 * KC)
        qkv_done = steps("qkv_done", 3 * NT)
        rot_parts = steps("rot_parts", 2 * NT)
        rot_ready = steps("rot_ready", 2 * NT)
        vs_ready = steps("vs_ready", NT)
        sq_ready = steps("sq_ready", 2 * NT)
        sq_used = steps("sq_used", 2 * NT)
        sums_ready = steps("sums_ready", 1)
        norms_ready = steps("norms_ready", 1)
        qk_scaled = steps("qk_scaled", 2 * NT)
        qk_tr = steps("qk_tr", 3 * NT)
        q_turned = steps("q_turned", 2 * NT)
        k_turned = steps("k_turned", NT)
        hyp_done = steps("hyp_done", N_HYP * NT)
        arg_ready = steps("arg_ready", N_HYP * NT)
        arg1_ready = steps("arg1_ready", 1)
        hyp_sq_ready = steps("hyp_sq_ready", 1)
        hyp_root_ready = steps("hyp_root_ready", 1)
        hyp_sum_ready = steps("hyp_sum_ready", 1)
        hyp_ln_ready = steps("hyp_ln_ready", 1)
        hyp_scaled = steps("hyp_scaled", 1)
        s_done = steps("s_done", N_SDOT)
        s_shifted = steps("s_shifted", NU)
        p_ready = steps("p_ready", NU)
        p_tr = steps("p_tr", NU)
        pt_ready = steps("pt_ready", NU)
        pv_done = steps("pv_done", NU)
        sum_tr = steps("sum_tr", 2)
        inv_ready = steps("inv_ready", 2)
        inv_spread_done = steps("inv_spread_done", 2 * NT)
        proj_done = steps("proj_done", 2 * NT)
        x1_ready = steps("x1_ready", NT)
        x1b_ready = steps("x1b_ready", 1)
        v_done = steps("v_done", NC)
        v_ready = steps("v_ready", NC)
        q2_done = steps("q2_done", KC)
        q2_ready = [steps(f"q2_ready{i}", KC // 2) for i in range(2)]
        cs_done = steps("cs_done", NU)
        cs_masked = steps("cs_masked", NU)
        cs_shifted = steps("cs_shifted", NU)
        cp_ready = steps("cp_ready", NU)
        cp_tr = steps("cp_tr", 2 * NU)
        cpt_ready = steps("cpt_ready", 2 * NU)
        cpv_done = steps("cpv_done", NU)
        x2_ready = steps("x2_ready", NT)
        x2_stored = steps("x2_stored", 16)

        def out_t(t, h):
            return ps_o[t][HD * (h % 4):HD * (h % 4 + 1), (h // 4) * TT:(h // 4 + 1) * TT]

        x_v = a["x"].rearrange("b (t p) d -> b p t d", p=TT)
        x2_v = x2_dram.rearrange("(b t p) d -> b p t d", p=TT, t=NT)
        ctx_v = a["ctx_t"].rearrange("b (c p) s -> b p c s", p=P)

        def batch_of(view, b):
            return view[bass.ds(b, 1)].rearrange("o p t d -> (o p) t d")

        block = ctx.enter_context(nc.Block())

        @block.sync
        def _(sp):
            def weight(dst, src, loaded):
                sp.dma_start(dst[:], src.rearrange("(c p) n -> p c n", p=P)).then_inc(loaded, 16)

            sp.dma_start(x_in[:], batch_of(x_v, 0)).then_inc(x_loaded.sem, 16)
            weight(w_k, a["wk"], w_k_in)
            sp.dma_start(ctx_t[:], batch_of(ctx_v, 0)).then_inc(ctx_loaded.sem, 16)
            weight(w_qkv, a["w_qkv_t"], w_qkv_in)
            for dst, src in ((w_v, "wv"), (w_proj, "w_proj_t"), (w_q, "wq"), (w_o, "wo")):
                weight(dst, a[src], weights_in)
            with sp.Fori(0, B - 1) as b:
                sp.wait_ge(xb_ready.sem, xb_ready.at(b, 1))
                sp.wait_ge(xn_ready.sem, xn_ready.at(b, NT))
                sp.dma_start(x_in[:], batch_of(x_v, b + 1)).then_inc(x_loaded.sem, 16)
                sp.wait_ge(v_done.sem, v_done.at(b, NC))
                sp.dma_start(ctx_t[:], batch_of(ctx_v, b + 1)).then_inc(ctx_loaded.sem, 16)

        @block.tensor
        def _(pe):
            def k_group(b, g, n):
                c, part = g // 2, g % 2
                for kc in range(KC):
                    mm = nc.tensor.matmul(bank[n % 4][:, 0:HC], w_k[:, kc, c * P:(c + 1) * P],
                                          ctx_t[:, kc, part * HC:(part + 1) * HC],
                                          start=(kc == 0), stop=(kc == KC - 1))
                mm.then_inc(k_done.sem, 1)

            def act_transpose(b, t):
                for c in range(KC):
                    mm = nc.tensor.transpose(ps_t[t][:, c * TT:(c + 1) * TT], x_n[:, t, c * P:(c + 1) * P],
                                             ident[0:TT, 0:TT])
                mm.then_inc(act_tr.sem, 1)

            def spread_sums(b, k):
                pe.wait_ge(inv_ready.sem, inv_ready.at(b, k + 1))
                for t in range(NT):
                    for c in range(KC):
                        mm = nc.tensor.matmul(ps_t[t][:, c * TT:(c + 1) * TT], head_rows[:, t * KC + c, :], inv_sum[:],
                                              start=True, stop=True)
                    mm.then_inc(inv_spread_done.sem, 1)

            def project(out, w, t, done):
                for kc in range(KC):
                    mm = nc.tensor.matmul(out[0:TT, :], act_t[:, kc, t * TT:(t + 1) * TT], w[:, kc, :],
                                          start=(kc == 0), stop=(kc == KC - 1))
                mm.then_inc(done.sem, 1)

            def v_step(b, m):
                j, kc = m // KC, m % KC
                if kc == 0:
                    if j < 2:
                        pe.wait_ge(arg_ready.sem, arg_ready.at(b, N_HYP * NT))
                    else:
                        pe.wait_ge(v_ready.sem, v_ready.at(b, j - 1))
                mm = nc.tensor.matmul(bank[2 + j % 2][0:CT, :], ctx_t[:, kc, j * CT:(j + 1) * CT], w_v[:, kc, :],
                                      start=(kc == 0), stop=(kc == KC - 1))
                if kc == KC - 1:
                    mm.then_inc(v_done.sem, 1)

            pe.wait_ge(w_k_in, 16)
            pe.wait_ge(pool_consts, 3)
            with pe.Fori(0, B) as b:
                pe.wait_ge(ctx_loaded.sem, ctx_loaded.at(b, 16))
                for g in range(4):
                    k_group(b, g, g)
                for t in range(NT):
                    pe.wait_ge(xn_ready.sem, xn_ready.at(b, t + 1))
                    act_transpose(b, t)
                pe.wait_ge(w_qkv_in, 16)
                for j in range(3 * NT):
                    t, part = j // 3, j % 3
                    if part == 0:
                        pe.wait_ge(act_ready.sem, act_ready.at(b, t + 1))
                    if j < 4:
                        pe.wait_ge(k_ready.sem, k_ready.at(b, j + 1))
                    else:
                        pe.wait_ge(rot_parts.sem, rot_parts.at(b, j - 3))
                    for kc in range(KC):
                        mm = nc.tensor.matmul(bank[j % 4][0:TT, :], act_t[:, kc, t * TT:(t + 1) * TT],
                                              w_qkv[:, kc, part * D:(part + 1) * D],
                                              start=(kc == 0), stop=(kc == KC - 1))
                    mm.then_inc(qkv_done.sem, 1)
                for g, last in zip(range(4, 7), ((vs_ready, 1), (rot_parts, 3), (rot_parts, 4))):
                    pe.wait_ge(last[0].sem, last[0].at(b, last[1]))
                    k_group(b, g, g + 2)
                for g in range(3 * NT):
                    t, r = g // 3, g % 3
                    if g == 3:
                        pe.wait_ge(vs_ready.sem, vs_ready.at(b, 2))
                        k_group(b, 7, 9)
                    pe.wait_ge(qk_scaled.sem, qk_scaled.at(b, 2 * t + min(r, 1) + 1))
                    if g >= 2:
                        t0, r0 = (g - 2) // 3, (g - 2) % 3
                        if r0 == 1:
                            pe.wait_ge(k_turned.sem, k_turned.at(b, t0 + 1))
                        else:
                            pe.wait_ge(q_turned.sem, q_turned.at(b, 2 * t0 + r0 // 2 + 1))
                    for c in range(KC if r < 2 else 2):
                        src = qk[:, 2 * t + r, c * P:(c + 1) * P] if r < 2 else qk[:, 2 * t + c, D:D + P]
                        mm = nc.tensor.transpose(ps_t[g % 2][:, c * TT:(c + 1) * TT], src, ident[0:TT, 0:TT])
                    mm.then_inc(qk_tr.sem, 1)
                pe.wait_ge(q_turned.sem, q_turned.at(b, 2 * NT))
                pe.wait_ge(k_turned.sem, k_turned.at(b, NT))
                pe.wait_ge(k_ready.sem, k_ready.at(b, 2 * KC))
                for g in range(N_HYP * NT):
                    t, hh = g // N_HYP, g % N_HYP
                    nk = (t + 1) * TT
                    if g >= N_HYP:
                        pe.wait_ge(arg_ready.sem, arg_ready.at(b, g - N_HYP + 1))
                    for c in (KC - 1, KC):
                        mm = nc.tensor.matmul(bank[hh][0:TT, 0:nk], q_m[:, 4 * c + hh, t * TT:(t + 1) * TT],
                                              keys_t[:, c, 0:nk], start=(c == KC - 1), stop=(c == KC))
                    mm.then_inc(hyp_done.sem, 1)

                def scores(u):
                    t, h = UNITS[u]
                    nk = (t + 1) * TT
                    if u < 2:
                        pe.wait_ge(arg_ready.sem, arg_ready.at(b, N_HYP + u + 1))
                    else:
                        pe.wait_ge(s_shifted.sem, s_shifted.at(b, u - 1))
                    nc.tensor.matmul(bank[u % 2][0:TT, 0:nk], q_m[:, h, t * TT:(t + 1) * TT],
                                     keys_t[:, h // 4, 0:nk], start=True, stop=True).then_inc(s_done.sem, 1)

                def turn(u):
                    t, h = UNITS[u]
                    pe.wait_ge(p_ready.sem, p_ready.at(b, u + 1))
                    if u >= 2:
                        pe.wait_ge(pt_ready.sem, pt_ready.at(b, u - 1))
                    for j in range(t + 1):
                        mm = nc.tensor.transpose(ps_t[u % 2][0:TT, j * TT:(j + 1) * TT],
                                                 prob[:, u % 3, j * TT:(j + 1) * TT], ident[0:TT, 0:TT])
                    mm.then_inc(p_tr.sem, 1)

                def weigh(u):
                    t, h = UNITS[u]
                    pe.wait_ge(pt_ready.sem, pt_ready.at(b, u + 1))
                    for j in range(t + 1):
                        mm = nc.tensor.matmul(out_t(t, h), v_s[:, j, h * HD:(h + 1) * HD],
                                              prob_t[0:TT, u % 2, j * TT:(j + 1) * TT], start=(j == 0), stop=(j == t))
                    mm.then_inc(pv_done.sem, 1)

                pe.wait_ge(vs_ready.sem, vs_ready.at(b, NT))
                pe.wait_ge(weights_in, 16 * 4)
                for u in range(NU + 4):
                    if u < N_SDOT:
                        scores(u)
                    if 3 <= u < NU + 3:
                        turn(u - 3)
                    if V_FROM <= u < V_FROM + KC * V_SELF:
                        v_step(b, u - V_FROM)
                    if u >= 4:
                        weigh(u - 4)
                pe.wait_ge(p_ready.sem, p_ready.at(b, NU))
                nc.tensor.transpose(ps_t[0][0:NU, 0:TT], row_sum[:], ident[0:TT, 0:TT]).then_inc(sum_tr.sem, 1)
                for m in range(KC * V_SELF, KC * min(NC, V_SELF + 1)):
                    v_step(b, m)
                spread_sums(b, 0)
                for t in range(NT):
                    pe.wait_ge(act_ready.sem, act_ready.at(b, NT + t + 1))
                    project(ps_o[t], w_proj, t, proj_done)
                for m in range(KC * (V_SELF + 1), KC * NC):
                    v_step(b, m)
                for t in range(NT):
                    pe.wait_ge(xn_ready.sem, xn_ready.at(b, NT + t + 1))
                    act_transpose(b, t)
                pe.wait_ge(act_ready.sem, act_ready.at(b, 3 * NT))
                pe.wait_ge(v_ready.sem, v_ready.at(b, NC))
                for c in range(KC):
                    for kc in range(KC):
                        mm = nc.tensor.matmul(bank[c][:, 0:S], w_q[:, kc, c * P:(c + 1) * P], act_t[:, kc, :],
                                              start=(kc == 0), stop=(kc == KC - 1))
                    mm.then_inc(q2_done.sem, 1)

                def cross_scores(u):
                    t, h = u // H, u % H
                    if u >= 2:
                        pe.wait_ge(cs_masked.sem, cs_masked.at(b, u - 1))
                    for part in range(2):
                        mm = nc.tensor.matmul(ps_s[u % 2][0:TT, part, 0:HC], q_m[:, h, t * TT:(t + 1) * TT],
                                              k_t[:, h // 4, part * HC:(part + 1) * HC], start=True, stop=True)
                    mm.then_inc(cs_done.sem, 1)

                def cross_turn(u):
                    pe.wait_ge(cp_ready.sem, cp_ready.at(b, u + 1))
                    for i in range(2):
                        if u >= 1:
                            pe.wait_ge(cpt_ready.sem, cpt_ready.at(b, 2 * u - 1 + i))
                        for j in range(3):
                            o = (3 * i + j) * CT
                            mm = nc.tensor.transpose(ps_t[i][0:CT, j * TT:(j + 1) * TT], prob[:, u % 3, o:o + CT],
                                                     ident[0:TT, 0:TT])
                        mm.then_inc(cp_tr.sem, 1)

                def cross_weigh(u):
                    t, h = u // H, u % H
                    for j in range(NC):
                        if j % 3 == 0:
                            pe.wait_ge(cpt_ready.sem, cpt_ready.at(b, 2 * u + j // 3 + 1))
                        mm = nc.tensor.matmul(out_t(t, h), v_c[:, j, h * HD:(h + 1) * HD],
                                              prob_t[0:CT, u % 2, j * TT:(j + 1) * TT], start=(j == 0),
                                              stop=(j == NC - 1))
                    mm.then_inc(cpv_done.sem, 1)

                for ready in q2_ready:
                    pe.wait_ge(ready.sem, ready.at(b, KC // 2))
                for u in range(NU + 3):
                    if u < NU:
                        cross_scores(u)
                    if 2 <= u < NU + 2:
                        cross_turn(u - 2)
                    if u >= 3:
                        cross_weigh(u - 3)
                nc.tensor.transpose(ps_t[0][0:NU, 0:TT], row_sum[:], ident[0:TT, 0:TT]).then_inc(sum_tr.sem, 1)
                spread_sums(b, 1)
                for t in range(NT):
                    pe.wait_ge(act_ready.sem, act_ready.at(b, 3 * NT + t + 1))
                    project(ps_o[t], w_o, t, proj_done)

        @block.vector
        def _(dve):
            dve.wait_ge(tables_in, 16 * 9)
            nc.vector.tensor_scalar(mask_bias[:], mask[:], -1.0, 1.0, ALU.mult, ALU.add)
            nc.vector.memset(factor[:], 1.0)
            nc.vector.memset(qk[:], 0.0)
            nc.vector.memset(minus_half[:], -0.5)
            nc.vector.memset(norm_add[:], 0.0)
            nc.vector.tensor_scalar(neg_curv[:], curv[:], -1.0, None, ALU.mult)
            nc.vector.reciprocal(inv_curv[:], curv[:])
            nc.vector.drain()
            nc.vector.tensor_scalar(mask_bias[:], mask_bias[:], -1.0e10, None, ALU.mult)
            nc.vector.tensor_copy(norm_add[:, N_COS:], inv_curv[0:TT, :])
            nc.vector.memset(factor[:, 0:2 * NT:2, 0:N_SDPA], 1.0 / SQRT_HD)
            nc.vector.drain().then_inc(consts, 1)

            def norm(b, src, k):
                for t in range(NT):
                    nc.vector.bn_stats(stats[:, t, :], src[:, t, :])
                nc.vector.drain()
                for t in range(NT):
                    nc.vector.bn_aggr(mean_var[:, t, :], stats[:, t, :])
                nc.vector.drain()
                nc.vector.tensor_scalar(var_eps[:], mean_var[:, :, 1], LN_EPS, None, ALU.add)\
                    .then_inc(var_ready.sem, 1)
                dve.wait_ge(rstd_ready.sem, rstd_ready.at(b, k + 1))
                for t in range(NT):
                    nc.vector.tensor_scalar(x_n[:, t, :], src[:, t, :], mean_var[:, t, 0:1], rstd[:, t:t + 1],
                                            ALU.subtract, ALU.mult).then_inc(xn_ready.sem, 1)

            def act_out(b, k, t):
                dve.wait_ge(act_tr.sem, act_tr.at(b, NT * k + t + 1))
                nc.vector.tensor_copy(act_t[:, :, t * TT:(t + 1) * TT],
                                      ps_t[t][:, 0:KC * TT].rearrange("p (c n) -> p c n", c=KC))\
                    .then_inc(act_ready.sem, 1)

            def v_out(b, j):
                dve.wait_ge(v_done.sem, v_done.at(b, j + 1))
                nc.vector.tensor_tensor(v_c[:, j, :], bank[2 + j % 2][0:CT, :], bv[0:CT, :], ALU.add)\
                    .then_inc(v_ready.sem, 1)

            def inverses(b, k):
                dve.wait_ge(sum_tr.sem, sum_tr.at(b, k + 1))
                nc.vector.reciprocal(inv_sum[:], ps_t[0][0:NU, 0:TT]).then_inc(inv_ready.sem, 1)

            def outputs(b, k):
                for t in range(NT):
                    dve.wait_ge(inv_spread_done.sem, inv_spread_done.at(b, NT * k + t + 1))
                    nc.vector.tensor_copy(inv_spread[:, t, :], ps_t[t][:, 0:KC * TT])
                nc.vector.drain()
                for t in range(NT):
                    nc.vector.tensor_tensor(act_t[:, :, t * TT:(t + 1) * TT],
                                            ps_o[t][:, 0:KC * TT].rearrange("p (c n) -> p c n", c=KC),
                                            inv_spread[:, t, :].rearrange("p (c n) -> p c n", c=KC), ALU.mult)\
                        .then_inc(act_ready.sem, 1)

            with dve.Fori(0, B) as b:
                dve.wait_ge(x_loaded.sem, x_loaded.at(b, 16))
                norm(b, x_in, 0)
                for t in range(NT):
                    act_out(b, 0, t)
                for r in range(2 * NT):
                    t, part = r // 2, r % 2
                    j = 3 * t + part
                    dve.wait_ge(qkv_done.sem, qkv_done.at(b, j + 1))
                    if r >= 2:
                        dve.wait_ge(rot_ready.sem, rot_ready.at(b, r - 1))
                    src = bank[j % 4][0:TT, :].rearrange("p (h s d) -> p h s d", h=H, s=2)
                    parts = rot_b[:, part, :].rearrange("p (h s d) -> p h s d", h=H, s=2)
                    nc.vector.tensor_tensor(rot_a[:, part, :].rearrange("p (h d) -> p h d", h=H),
                                            bank[j % 4][0:TT, :].rearrange("p (h d) -> p h d", h=H),
                                            spread(rot_cos[:, t, :], 1, H), ALU.mult)
                    for s in range(2):
                        last = nc.vector.tensor_tensor(parts[:, :, s, :], src[:, :, 1 - s, :],
                                                       spread(rot_sin[:, t, s * HD // 2:(s + 1) * HD // 2], 1, H),
                                                       ALU.mult)
                    last.then_inc(rot_parts.sem, 1)
                for r in range(2 * NT):
                    dve.wait_ge(sq_ready.sem, sq_ready.at(b, r + 1))
                    nc.vector.tensor_reduce(sums[:, r, :], squares[:, r % 2, :].rearrange("p (h d) -> p h d", d=HD),
                                            AX_X, ALU.add).then_inc(sq_used.sem, 1)
                nc.vector.drain()
                nc.vector.tensor_tensor(sums[:], sums[:], spread(norm_add[:], 1, 2 * NT), ALU.add)\
                    .then_inc(sums_ready.sem, 1)
                dve.wait_ge(norms_ready.sem, norms_ready.at(b, 1))
                nc.vector.tensor_scalar(sums[:, :, 0:N_COS], norms[:, :, 0:N_COS], 1e-12, None, ALU.max)
                times = qk[:, :, D:].rearrange("p r (h d) -> p r h d", d=HD)
                nc.vector.tensor_copy(times[:, 0:2 * NT:2, :, 0], norms[:, 0:2 * NT:2, N_COS:])
                nc.vector.tensor_scalar(times[:, 1:2 * NT:2, :, 0], norms[:, 1:2 * NT:2, N_COS:], -1.0, None, ALU.mult)
                nc.vector.drain()
                nc.vector.reciprocal(factor[:, :, N_SDPA:N_DOT], sums[:, :, 0:N_COS])
                nc.vector.drain()
                nc.vector.tensor_scalar(factor[:, 0:2 * NT:2, N_SDPA:N_DOT], factor[:, 0:2 * NT:2, N_SDPA:N_DOT],
                                        SQRT_HD, None, ALU.mult)
                nc.vector.drain()
                for r in range(2 * NT):
                    view = qk[:, r, 0:D].rearrange("p (h d) -> p h d", h=H)
                    nc.vector.tensor_tensor(view, view, spread(factor[:, r, :], 2, HD), ALU.mult)\
                        .then_inc(qk_scaled.sem, 1)
                for t in range(NT):
                    dve.wait_ge(qk_tr.sem, qk_tr.at(b, 3 * t + 2))
                    nc.vector.tensor_copy(keys_t[:, 0:KC, t * TT:(t + 1) * TT],
                                          ps_t[(3 * t + 1) % 2][:, 0:KC * TT].rearrange("p (c n) -> p c n", n=TT))\
                        .then_inc(k_turned.sem, 1)
                for g in range(N_HYP * NT):
                    t, hh = g // N_HYP, g % N_HYP
                    nk = (t + 1) * TT
                    dve.wait_ge(hyp_done.sem, hyp_done.at(b, g + 1))
                    nc.vector.tensor_scalar(hyp_part(arg, t, hh), by_tile(bank[hh][0:TT, 0:nk]),
                                            neg_curv[0:TT, hh:hh + 1], 1.0 + 1e-7, ALU.mult, ALU.max)\
                        .then_inc(arg_ready.sem, 1)

                def shift(u):
                    t, h = UNITS[u]
                    nk, off = (t + 1) * TT, t * TT
                    if u < N_SDOT:
                        dve.wait_ge(s_done.sem, s_done.at(b, u + 1))
                        src = by_tile(bank[u % 2][0:TT, 0:nk])
                    else:
                        src = hyp_part(hyp, t, h - N_DOT)
                    if u >= 3:
                        dve.wait_ge(p_ready.sem, p_ready.at(b, u - 2))
                    dve.sem_inc(passed_dve, 1)
                    nc.vector.tensor_tensor_reduce(by_tile(neg_s[:, u % 3, 0:nk]), src,
                                                   by_tile(causal[:, off:off + nk]), -1.0, 3.4e38,
                                                   ALU.add, ALU.min, neg_max[:, u:u + 1]).then_inc(s_shifted.sem, 1)

                def turned(u):
                    t, h = UNITS[u]
                    nk = (t + 1) * TT
                    dve.wait_ge(p_tr.sem, p_tr.at(b, u + 1))
                    if u >= 2:
                        dve.wait_ge(pv_done.sem, pv_done.at(b, u - 1))
                    nc.vector.tensor_copy(prob_t[0:TT, u % 2, 0:nk], ps_t[u % 2][0:TT, 0:nk])\
                        .then_inc(pt_ready.sem, 1)

                for u in range(NU + 3):
                    if u == 7:
                        dve.wait_ge(arg1_ready.sem, arg1_ready.at(b, 1))
                        nc.vector.scalar_tensor_tensor(hyp, arg, -1.0, hyp, ALU.add, ALU.mult)\
                            .then_inc(hyp_sq_ready.sem, 1)
                    if RECIP_AT <= u < RECIP_AT + 6:
                        i = u - RECIP_AT
                        if i == 0:
                            dve.wait_ge(hyp_scaled.sem, hyp_scaled.at(b, 1))
                        part = hyp[:, i // 2, (i % 2) * 2 * TT:(i % 2 + 1) * 2 * TT]
                        nc.vector.reciprocal(part, part)
                        if i % 2 == 1:
                            nc.vector.drain()
                    if u >= V_FROM + KC + 1 and (u - V_FROM - 1) % KC == 0 and (u - V_FROM - 1) // KC <= V_SELF:
                        v_out(b, (u - V_FROM - 1) // KC - 1)
                    if u < NU:
                        shift(u)
                    if u >= 3:
                        turned(u - 3)
                dve.wait_ge(pv_done.sem, pv_done.at(b, NU))
                inverses(b, 0)
                if V_SELF < NC:
                    v_out(b, V_SELF)
                outputs(b, 0)
                dve.wait_ge(xb_ready.sem, xb_ready.at(b, 1))
                dve.wait_ge(x2_stored.sem, x2_stored.at(b, 16))
                for t in range(NT):
                    dve.wait_ge(proj_done.sem, proj_done.at(b, t + 1))
                    nc.vector.tensor_tensor(x1[:, t, :], ps_o[t][0:TT, :], x_b[:, t, :], ALU.add)\
                        .then_inc(x1_ready.sem, 1)
                nc.vector.drain()
                norm(b, x1, 1)
                for j in range(V_SELF + 1, NC):
                    v_out(b, j)
                for t in range(NT):
                    act_out(b, 1, t)
                for c in range(1, KC, 2):
                    dve.wait_ge(q2_done.sem, q2_done.at(b, c + 1))
                    for i in range(4):
                        rows = slice(HD * i, HD * (i + 1))
                        last = nc.vector.tensor_scalar(q_m[rows, 4 * c + i, :], bank[c][rows, 0:S], bq[rows, c:c + 1],
                                                       None, ALU.add)
                    last.then_inc(q2_ready[1].sem, 1)

                def masked(u):
                    t = u // H
                    dve.wait_ge(cs_done.sem, cs_done.at(b, u + 1))
                    if u >= 3:
                        dve.wait_ge(cp_ready.sem, cp_ready.at(b, u - 2))
                    nc.vector.scalar_tensor_tensor(neg_s[:, u % 3, :].rearrange("p (i n) -> p i n", i=2),
                                                   ps_s[u % 2][0:TT, :, 0:HC], 1.0 / SQRT_HD,
                                                   mask[:, t, :].rearrange("p (i n) -> p i n", i=2),
                                                   ALU.mult, ALU.mult).then_inc(cs_masked.sem, 1)

                def shifted(u):
                    t = u // H
                    dve.wait_ge(cs_masked.sem, cs_masked.at(b, u + 1))
                    dve.sem_inc(passed_dve, 1)
                    nc.vector.tensor_tensor_reduce(neg_s[:, u % 3, :], neg_s[:, u % 3, :], mask_bias[:, t, :], -1.0, 3.4e38,
                                                   ALU.add, ALU.min, neg_max[:, u:u + 1]).then_inc(cs_shifted.sem, 1)

                for u in range(NU):
                    masked(u)
                    shifted(u)
                inverses(b, 1)
                outputs(b, 1)
                dve.wait_ge(x1b_ready.sem, x1b_ready.at(b, 1))
                for t in range(NT):
                    dve.wait_ge(proj_done.sem, proj_done.at(b, NT + t + 1))
                    nc.vector.tensor_tensor(x2[:, t, :], ps_o[t][0:TT, :], x_b[:, t, :], ALU.add)\
                        .then_inc(x2_ready.sem, 1)

        @block.scalar
        def _(act):
            for dst, src in ((mask, a["mask"].rearrange("(t p) s -> p t s", p=TT)),
                             (curv, a["curv"]), (rot_cos, a["rot_cos"].rearrange("(t p) d -> p t d", p=TT)),
                             (rot_sin, a["rot_sin"].rearrange("(t p) d -> p t d", p=TT)),
                             (bk, a["bk"]), (bq, a["bq"]),
                             (proj_b, a["proj_b"].partition_broadcast(P)), (bv, a["bv"].partition_broadcast(P)),
                             (bo, a["bo"].partition_broadcast(P))):
                act.dma_start(dst[:], src).then_inc(tables_in, 16)
            act.sem_inc(x2_stored.sem, 16)
            act.wait_ge(consts, 1)
            nc.scalar.activation(root_inv_curv[:], inv_curv[:], ACT.Sqrt)

            def k_out(b, g, n):
                act.wait_ge(k_done.sem, k_done.at(b, g + 1))
                c, part = g // 2, g % 2
                nc.scalar.activation(k_t[:, c, part * HC:(part + 1) * HC], bank[n % 4][:, 0:HC], ACT.Identity,
                                     bias=bk[:, c:c + 1]).then_inc(k_ready.sem, 1)

            nc.scalar.drain().then_inc(consts, 1)
            with act.Fori(0, B) as b:
                for g in range(4):
                    k_out(b, g, g)
                for t in range(NT):
                    j = 3 * t + 2
                    act.wait_ge(qkv_done.sem, qkv_done.at(b, j + 1))
                    nc.scalar.copy(v_s[:, t, :], bank[j % 4][0:TT, :]).then_inc(vs_ready.sem, 1)
                k_out(b, 4, 6)
                act.wait_ge(sums_ready.sem, sums_ready.at(b, 1))
                nc.scalar.activation(norms[:], sums[:], ACT.Sqrt).then_inc(norms_ready.sem, 1)
                for g in range(5, 7):
                    k_out(b, g, g + 2)

                for g in range(3 * NT):
                    t, r = g // 3, g % 3
                    if r == 1:
                        continue
                    if g == 3:
                        k_out(b, 7, 9)
                    act.wait_ge(qk_tr.sem, qk_tr.at(b, g + 1))
                    cols = slice(t * TT, (t + 1) * TT)
                    for i in range(4):
                        rows = slice(HD * i, HD * (i + 1))
                        dst = q_m[rows, i:H:4, cols] if r == 0 else q_m[rows, H + i:H + i + 1, cols]
                        n = KC if r == 0 else 1
                        last = nc.scalar.copy(dst, ps_t[g % 2][rows, 0:n * TT].rearrange("p (c n) -> p c n", n=TT))
                    if r == 2:
                        last = nc.scalar.copy(keys_t[:, KC, cols], ps_t[g % 2][:, TT:2 * TT])
                    last.then_inc(q_turned.sem, 1)
                for u in range(NU):
                    t, h = UNITS[u]
                    nk = (t + 1) * TT
                    if u == ROOT_AT:
                        act.wait_ge(hyp_sq_ready.sem, hyp_sq_ready.at(b, 1))
                        nc.scalar.activation(hyp, hyp, ACT.Sqrt).then_inc(hyp_root_ready.sem, 1)
                    if u == LN_AT:
                        act.wait_ge(hyp_sum_ready.sem, hyp_sum_ready.at(b, 1))
                        nc.scalar.activation(hyp, hyp, ACT.Ln).then_inc(hyp_ln_ready.sem, 1)
                    act.wait_ge(s_shifted.sem, s_shifted.at(b, u + 1))
                    if u >= 3:
                        act.wait_ge(p_tr.sem, p_tr.at(b, u - 2))
                    nc.scalar.activation(prob[:, u % 3, 0:nk], neg_s[:, u % 3, 0:nk], ACT.Exp,
                                         bias=neg_max[:, u:u + 1], scale=-1.0,
                                         accum_out=row_sum[:, t * H + h:t * H + h + 1]).then_inc(p_ready.sem, 1)
                for c in range(0, KC, 2):
                    act.wait_ge(q2_done.sem, q2_done.at(b, c + 1))
                    for i in range(4):
                        rows = slice(HD * i, HD * (i + 1))
                        last = nc.scalar.activation(q_m[rows, 4 * c + i, :], bank[c][rows, 0:S], ACT.Identity,
                                                    bias=bq[rows, c:c + 1])
                    last.then_inc(q2_ready[0].sem, 1)

                def cross_exp(u):
                    act.wait_ge(cs_shifted.sem, cs_shifted.at(b, u + 1))
                    if u >= 3:
                        act.wait_ge(cp_tr.sem, cp_tr.at(b, 2 * u - 4))
                    nc.scalar.activation(prob[:, u % 3, :], neg_s[:, u % 3, :], ACT.Exp, bias=neg_max[:, u:u + 1],
                                         scale=-1.0, accum_out=row_sum[:, u:u + 1]).then_inc(cp_ready.sem, 1)

                def cross_turned(u):
                    for i in range(2):
                        act.wait_ge(cp_tr.sem, cp_tr.at(b, 2 * u + i + 1))
                        if u >= 2 and i == 0:
                            act.wait_ge(cpv_done.sem, cpv_done.at(b, u - 1))
                        nc.scalar.copy(prob_t[0:CT, u % 2, i * HB:(i + 1) * HB], ps_t[i][0:CT, 0:HB])\
                            .then_inc(cpt_ready.sem, 1)

                for u in range(NU + 2):
                    if u >= 2:
                        cross_turned(u - 2)
                    if u < NU:
                        cross_exp(u)
                act.wait_ge(x2_ready.sem, x2_ready.at(b, NT))
                act.dma_start(batch_of(x2_v, b), x2[:]).then_inc(x2_stored.sem, 16)
            act.wait_ge(x2_stored.sem, 16 * (B + 1))

        @block.gpsimd
        def _(pool):
            nc.gpsimd.memset(ident[:], 0.0)
            nc.gpsimd.memset(head_rows[:], 0.0)
            nc.gpsimd.memset(q_m[:], 0.0)
            nc.gpsimd.memset(causal[:], 0.0).then_inc(pool_consts, 1)
            pool.wait_ge(pool_consts, 1)
            nc.gpsimd.affine_select(out=ident[:], in_=ident[:], compare_op=ALU.not_equal, fill=1.0, base=0,
                                    pattern=[[-1, P]], channel_multiplier=1).then_inc(pool_consts, 1)
            nc.gpsimd.affine_select(out=head_rows[:].rearrange("r k (g d) -> r k g d", d=HD),
                                    in_=head_rows[:].rearrange("r k (g d) -> r k g d", d=HD),
                                    compare_op=ALU.not_equal, fill=1.0, base=0,
                                    pattern=[[-4, NT * KC], [-1, 4], [0, HD]], channel_multiplier=1)
            nc.gpsimd.affine_select(out=causal[:, 0:TT], in_=causal[:, 0:TT], compare_op=ALU.is_ge, fill=NEG, base=0,
                                    pattern=[[-1, TT]], channel_multiplier=1)
            nc.gpsimd.affine_select(out=causal[:, TT:], in_=causal[:, TT:], compare_op=ALU.is_ge, fill=NEG, base=TT,
                                    pattern=[[-1, S]], channel_multiplier=1).then_inc(pool_consts, 1)
            pool.wait_ge(consts, 2)
            with pool.Fori(0, B) as b:
                def root(k):
                    pool.wait_ge(var_ready.sem, var_ready.at(b, k + 1))
                    nc.gpsimd.tensor_tensor(rstd[:], var_eps[:], minus_half[:], ALU.pow).then_inc(rstd_ready.sem, 1)

                root(0)
                nc.gpsimd.tensor_tensor(x_b[:], x_in[:], spread(proj_b[0:TT, :], 1, NT), ALU.add)\
                    .then_inc(xb_ready.sem, 1)
                for r in range(2 * NT):
                    pool.wait_ge(rot_parts.sem, rot_parts.at(b, r + 1))
                    nc.gpsimd.tensor_tensor(qk[:, r, 0:D], rot_a[:, r % 2, :], rot_b[:, r % 2, :], ALU.add)\
                        .then_inc(rot_ready.sem, 1)
                    pool.wait_ge(rot_ready.sem, rot_ready.at(b, r + 1))
                    if r >= 2:
                        pool.wait_ge(sq_used.sem, sq_used.at(b, r - 1))
                    heads = qk[:, r, N_SDPA * HD:D]
                    nc.gpsimd.tensor_tensor(squares[:, r % 2, :], heads, heads, ALU.mult).then_inc(sq_ready.sem, 1)
                pool.wait_ge(arg_ready.sem, arg_ready.at(b, N_HYP * NT))
                pool.sem_inc(passed_pool, 1)
                nc.gpsimd.tensor_scalar(hyp, arg, 1.0, None, ALU.add).then_inc(arg1_ready.sem, 1)
                pool.wait_ge(hyp_root_ready.sem, hyp_root_ready.at(b, 1))
                nc.gpsimd.tensor_tensor(hyp, hyp, arg, ALU.add).then_inc(hyp_sum_ready.sem, 1)
                pool.wait_ge(hyp_ln_ready.sem, hyp_ln_ready.at(b, 1))
                pool.sem_inc(passed_pool, 1)
                for hh in range(N_HYP):
                    part = hyp[:, :, hh * TT:(hh + 1) * TT]
                    last = nc.gpsimd.tensor_scalar(part, part, root_inv_curv[0:TT, hh:hh + 1], 1e-6, ALU.mult, ALU.add)
                last.then_inc(hyp_scaled.sem, 1)
                root(1)
                nc.gpsimd.tensor_tensor(x_b[:], x1[:], spread(bo[0:TT, :], 1, NT), ALU.add)\
                    .then_inc(x1b_ready.sem, 1)


HF = 8
KD = 128
NK = 128
TOP = 8
NF = 2 * HF
TOK = B * S
NTF = TOK // P
QC = 4
QN = TOK // QC
TPB = 4
NG = -(-NTF // TPB)
RING = 6
HU = TOP // 2
BN_EPS = 1e-5
PICK = NTF * TOP
GELU_C = (2.0 / 3.141592653589793) ** 0.5


def build_norm(nc, x2_dram, acc, xn_all, xn_t, ident):
    with ExitStack() as ctx:
        def sb(name, shape, dt=F32):
            return ctx.enter_context(nc.sbuf_tensor("n_" + name, shape, dt))

        def sem(name):
            return ctx.enter_context(nc.semaphore("n_" + name))

        xn = sb("xn", [P, 2, D])
        stats = sb("stats", [P, 6])
        mean_var = sb("mean_var", [P, 2])
        var_eps = sb("var_eps", [P, 1])
        rstd = sb("rstd", [P, 1])
        minus_half = sb("minus_half", [P, 1])
        ps_t = [ctx.enter_context(nc.psum_tensor(f"n_ps_t{i}", [P, 512], F32)) for i in range(2)]

        x_loaded = sem("x_loaded")
        normed = sem("normed")
        var_ready = sem("var_ready")
        rstd_ready = sem("rstd_ready")
        copied = sem("copied")
        turned = sem("turned")
        turned_out = sem("turned_out")
        half_ready = sem("half_ready")
        x2_v = x2_dram.rearrange("(n p) d -> p n d", p=P)

        block = ctx.enter_context(nc.Block())

        @block.sync
        def _(sp):
            for i in range(2):
                n = slice(0, 2) if i == 0 else slice(2, NTF)
                if i == 1:
                    sp.wait_ge(x_loaded, 16)
                sp.dma_start(acc[:, n, :], x2_v[:, n, :]).then_inc(x_loaded, 16)

        @block.gpsimd
        def _(pool):
            nc.gpsimd.memset(minus_half[:], -0.5).then_inc(half_ready, 1)
            pool.sem_inc(copied, 2)
            pool.wait_ge(half_ready, 1)
            with pool.Fori(0, NTF // 2) as i:
                for s in range(2):
                    pool.wait_ge(var_ready, 2 * i + s + 1)
                    nc.gpsimd.tensor_tensor(rstd[:], var_eps[:], minus_half[:], ALU.pow).then_inc(rstd_ready, 1)
                    pool.wait_ge(normed, 2 * i + s + 1)
                    nc.gpsimd.tensor_copy(xn_all[:, bass.ds(2 * i + s, 1), :].rearrange("p o d -> p (o d)"),
                                          xn[:, s, :]).then_inc(copied, 1)

        @block.tensor
        def _(pe):
            pe.sem_inc(turned, 2)
            with pe.Fori(0, NTF // 2) as i:
                for s in range(2):
                    pe.wait_ge(normed, 2 * i + s + 1)
                    pe.wait_ge(turned_out, 2 * i + s + 1)
                    for c in range(KC):
                        mm = nc.tensor.transpose(ps_t[s][:, c * P:(c + 1) * P], xn[:, s, c * P:(c + 1) * P], ident[:])
                    mm.then_inc(turned, 1)

        @block.vector
        def _(dve):
            def tile(n, s, view):
                nc.vector.bn_stats(stats[:], view)
                nc.vector.drain()
                nc.vector.bn_aggr(mean_var[:], stats[:])
                nc.vector.drain()
                nc.vector.tensor_scalar(var_eps[:], mean_var[:, 1:2], LN_EPS, None, ALU.add).then_inc(var_ready, 1)
                dve.wait_ge(copied, n + 1)
                dve.wait_ge(turned, n + 1)
                dve.wait_ge(rstd_ready, n + 1)
                nc.vector.tensor_scalar(xn[:, s, :], view, mean_var[:, 0:1], rstd[:], ALU.subtract, ALU.mult)\
                    .then_inc(normed, 1)

            dve.wait_ge(x_loaded, 16)
            for s in range(2):
                tile(s, s, acc[:, s, :])
            dve.wait_ge(x_loaded, 32)
            with dve.Fori(1, NTF // 2) as i:
                for s in range(2):
                    tile(2 * i + s, s, acc[:, bass.ds(2 * i + s, 1), :].rearrange("p o d -> p (o d)"))

        @block.scalar
        def _(act):
            act.sem_inc(turned_out, 2)
            with act.Fori(0, NTF // 2) as i:
                for s in range(2):
                    act.wait_ge(turned, 2 * i + s + 1 + 2)
                    nc.scalar.copy(xn_t[:, :, bass.ds((2 * i + s) * P, P)],
                                   ps_t[s][:].rearrange("p (c n) -> p c n", c=KC)).then_inc(turned_out, 1)


def build_experts(nc, a, out, acc, xn_all, xn_t, ident):
    with ExitStack() as ctx:
        def sb(name, shape, dt=F32):
            return ctx.enter_context(nc.sbuf_tensor("e_" + name, shape, dt))

        def psum(name, shape):
            return ctx.enter_context(nc.psum_tensor("e_" + name, shape, F32))

        def sem(name):
            return ctx.enter_context(nc.semaphore("e_" + name))

        rows = sb("rows", [P, RING, HU, 2 * D])
        w_q = sb("w_q", [P, 2, KC, KD])
        keys = sb("keys", [P, 2, NK])
        gamma = sb("gamma", [P, NF])
        beta = sb("beta", [P, NF])
        stats = sb("stats", [P, QC, 6])
        mean_var = sb("mean_var", [P, 2])
        var_eps = sb("var_eps", [P, 1])
        std = sb("std", [P, 1])
        rstd = sb("rstd", [P, 1])
        scale = sb("scale", [P, 1])
        shift = sb("shift", [P, 1])
        q_t = sb("q_t", [P, TOK])
        best = sb("best", [P, 2, NTF, TOP])
        best_at = sb("best_at", [P, 2, NTF, TOP], U32)
        best_at_f = sb("best_at_f", [P, 2, NTF, TOP])
        pair = q_t[:, 0:NTF * TOP * TOP].rearrange("p (t x y) -> p t x y", x=TOP, y=TOP)
        match = pair
        top = sb("top", [P, NTF, TOP])
        at = sb("at", [P, NTF, TOP], U32)
        at_xy = sb("at_xy", [P, 2, PICK], U32)
        at_f = sb("at_f", [P, 2, PICK])
        chosen = sb("chosen", [P, 2, PICK])
        eight = sb("eight", [P, TOP])
        soft = sb("soft", [P, NTF, TOP])
        soft_sum = sb("soft_sum", [P, NTF])
        idx_next = sb("idx_next", [P, PICK], U32)
        gate_next = sb("gate_next", [P, PICK])
        idx = sb("idx", [P, PICK], U32)
        gate = sb("gate", [P, PICK])
        hidden = sb("hidden", [P, 2, TOP])
        cubic = sb("cubic", [P, 2, TOP])
        tanh = sb("tanh", [P, 2, TOP])
        weight = sb("weight", [P, 2, TOP])
        diag = sb("diag", [P, TOP, P])

        ps_q = [psum(f"ps_q{i}", [P, 512]) for i in range(QC)]
        ps_m = [psum(f"ps_m{i}", [P, 512]) for i in range(2)]
        ps_out = [psum(f"ps_out{i}", [P, 512]) for i in range(2)]

        small_in = sem("small_in")
        iota_ready = sem("iota_ready")
        w_loaded = [sem(f"w_loaded{s}") for s in range(2)]
        q_done = sem("q_done")
        bn_var = sem("bn_var")
        bn_std = sem("bn_std")
        affine_ready = sem("affine_ready")
        q_ready = sem("q_ready")
        sims_made = sem("sims_made")
        sims_ready = sem("sims_ready")
        searched = sem("searched")
        soft_in = sem("soft_in")
        soft_out = sem("soft_out")
        idx_ready = sem("idx_ready")
        idx_here = sem("idx_here")
        rows_in = [sem(f"rows_in{g}") for g in range(RING)]
        rows_used = sem("rows_used")
        cubic_ready = sem("cubic_ready")
        tanh_ready = sem("tanh_ready")
        weight_ready = sem("weight_ready")
        diag_ready = sem("diag_ready")
        acc_done = sem("acc_done")
        out_stored = sem("out_stored")
        passed_dve = sem("passed_dve")
        passed_pool = sem("passed_pool")

        def nth(head, half):
            return 2 * head + half

        def uses(slot):
            return (2 * NTF - 1 - slot) // RING + 1

        def first(head):
            return isinstance(head, int) and head == 0

        def group(g):
            return range(g * TPB, min(NTF, (g + 1) * TPB))

        PE_STEPS = {0: [("project", 0, 0)], 1: [("project", 0, 1)], 3: [("match", 0, 0)],
                    4: [("match", 0, 1), ("project", 1, 0)], 5: [("project", 1, 1)], 7: [("match", 1, 0)],
                    8: [("match", 1, 1)]}
        ACT_STEPS = {2: [("affine", 0, 0)], 3: [("match", 0, 0)], 4: [("match", 0, 1)], 6: [("affine", 1, 0)],
                     7: [("match", 1, 0)], 8: [("match", 1, 1)], 10: [("soften", 0, 0)]}
        DVE_STEPS = {2: [("affine", 0, 0)], 4: [("search", 0, 0)], 5: [("search", 0, 1)], 6: [("affine", 1, 0)],
                     8: [("search", 1, 0)], 9: [("search", 1, 1)], 10: [("pairs", 0, 0)], 11: [("choice", 0, 0)]}
        N_STEPS = 12

        def run_heads(eng, steps, start, unit, finish):
            for k in range(N_STEPS):
                steps(0, k)
            with eng.Fori(0, HF - 1) as h:
                start(h)
                for t in range(NTF):
                    unit(h, t, lambda: steps(h + 1, t))
                finish(h)
            start(HF - 1)
            for t in range(NTF):
                unit(HF - 1, t, lambda: None)
            finish(HF - 1)

        block = ctx.enter_context(nc.Block())

        @block.sync
        def _(sp):
            sp.dma_start(gamma[:], a["gamma"]).then_inc(small_in, 16)
            sp.dma_start(beta[:], a["beta"]).then_inc(small_in, 16)
            w_v = a["ffn_wq"].rearrange("(c p) (f n) -> f p c n", p=P, n=KD)
            k_v = a["keys_t"].rearrange("p (f n) -> f p n", n=NK)

            def block_in(head, half):
                f = head + half * HF
                src = w_v[bass.ds(f, 1)].rearrange("o p c n -> (o p) c n")
                sp.dma_start(w_q[:, half], src).then_inc(w_loaded[half], 16)
                src = k_v[bass.ds(f, 1)].rearrange("o p n -> (o p) n")
                sp.dma_start(keys[:, half], src).then_inc(w_loaded[half], 16)

            for half in range(2):
                block_in(0, half)
            with sp.Fori(0, HF - 1) as h:
                for half in range(2):
                    sp.wait_ge(sims_made, NG * nth(h, half) + NG)
                    block_in(h + 1, half)
            for t in range(NTF):
                sp.wait_ge(acc_done, NTF * (HF - 1) + t + 1 + 2)
                sp.dma_start(out.rearrange("b s d -> (b s) d")[t * P:(t + 1) * P, :], acc[:, t, :])\
                    .then_inc(out_stored, 16)
            sp.wait_ge(out_stored, 16 * NTF)

        @block.gpsimd
        def _(pool):
            nc.gpsimd.iota(eight[:], [[1, TOP]], channel_multiplier=0, allow_small_or_imprecise_dtypes=True)\
                .then_inc(iota_ready, 1)
            table = a["experts"]
            with pool.Fori(0, HF) as h:
                pool.wait_ge(idx_ready, h + 1)
                pool.sem_inc(passed_pool, 1)
                for v in range(2 * NTF):
                    if v % NTF == 0:
                        part = slice(v // NTF * PICK // 2, (v // NTF + 1) * PICK // 2)
                        nc.gpsimd.tensor_copy(idx[:, part], idx_next[:, part]).then_inc(idx_here, 1)
                        pool.wait_ge(idx_here, 2 * h + v // NTF + 1)
                    last = v - RING if v >= RING else v + (2 * NTF - 1 - v) // RING * RING - 2 * NTF
                    pool.wait_ge(rows_used, 2 * NTF * h + last + 1 + RING)
                    pool.sem_inc(passed_pool, 1)
                    for k in range(HU):
                        e = v * HU + k
                        pool.indirect_dma_start(rows[:, v % RING, k, :], None, table[:, :],
                                                bass.IndirectOffsetOnAxis(ap=idx[:, e:e + 1], axis=0))\
                            .then_inc(rows_in[v % RING], 16)

        @block.tensor
        def _(pe):
            def project(head, half, part):
                n = nth(head, half)
                if part == 0:
                    pe.wait_ge(w_loaded[half], 32 * head + 32)
                for c in range(part * QC // 2, (part + 1) * QC // 2):
                    if not (first(head) and half == 0):
                        pe.wait_ge(q_ready, QC * (n - 1) + c + 1)
                    for kc in range(KC):
                        mm = nc.tensor.matmul(ps_q[c][:, 0:QN], w_q[:, half, kc, :], xn_t[:, kc, c * QN:(c + 1) * QN],
                                              start=(kc == 0), stop=(kc == KC - 1))
                    mm.then_inc(q_done, 1)

            def match_keys(head, half, part):
                n = nth(head, half)
                if part == 0:
                    pe.wait_ge(q_ready, QC * n + QC)
                for g in (2 * part, 2 * part + 1):
                    if not (first(head) and half == 0 and g < 2):
                        pe.wait_ge(sims_ready, NG * n + g - 1)
                    for i in group(g):
                        mm = nc.tensor.matmul(ps_m[g % 2][:, (i % TPB) * NK:(i % TPB + 1) * NK],
                                              q_t[:, i * P:(i + 1) * P], keys[:, half, :], start=True, stop=True)
                    mm.then_inc(sims_made, 1)

            def steps(head, k):
                for stage, half, part in PE_STEPS.get(k, ()):
                    (project if stage == "project" else match_keys)(head, half, part)

            def weigh_rows(h, t):
                pe.wait_ge(acc_done, NTF * h + t + 1)
                for k in range(TOP):
                    pe.wait_ge(diag_ready, TOP * (NTF * h + t) + k + 1)
                    v = 2 * t + k // HU
                    mm = nc.tensor.matmul(ps_out[t % 2][:], diag[:, k, :], rows[:, v % RING, k % HU, D:],
                                          start=(k == 0), stop=(k == TOP - 1))
                    if k % HU == HU - 1:
                        mm.then_inc(rows_used, 1)

            def unit(h, t, step):
                step()
                if t >= 1:
                    weigh_rows(h, t - 1)

            pe.sem_inc(rows_used, RING)
            run_heads(pe, steps, lambda h: None, unit, lambda h: weigh_rows(h, NTF - 1))

        @block.vector
        def _(dve):
            def affine(head, half):
                n = nth(head, half)
                f = head + half * HF
                for c in range(QC):
                    dve.wait_ge(q_done, QC * n + c + 1)
                    nc.vector.bn_stats(stats[:, c, :], ps_q[c][:, 0:QN])
                nc.vector.drain()
                nc.vector.bn_aggr(mean_var[:], stats[:].rearrange("p c n -> p (c n)"))
                nc.vector.drain()
                nc.vector.tensor_scalar(var_eps[:], mean_var[:, 1:2], BN_EPS, None, ALU.add).then_inc(bn_var, 1)
                dve.wait_ge(bn_std, n + 1)
                nc.vector.reciprocal(rstd[:], std[:])
                nc.vector.drain()
                nc.vector.tensor_tensor(scale[:], rstd[:], gamma[:, bass.ds(f, 1)], ALU.mult)
                nc.vector.drain()
                nc.vector.tensor_tensor(shift[:], mean_var[:, 0:1], scale[:], ALU.mult)
                nc.vector.drain()
                nc.vector.tensor_tensor(shift[:], beta[:, bass.ds(f, 1)], shift[:], ALU.subtract)\
                    .then_inc(affine_ready, 1)

            def search(head, half, part):
                n = nth(head, half)
                dve.wait_ge(sims_ready, NG * n + 2 * part + 2)
                dve.sem_inc(passed_dve, 1)
                tiles = [*group(2 * part), *group(2 * part + 1)]
                for i in tiles:
                    nc.vector.max(best[:, half, i, :], q_t[:, i * NK:(i + 1) * NK])
                nc.vector.drain()
                for i in tiles:
                    last = nc.vector.max_index(best_at[:, half, i, :], best[:, half, i, :], q_t[:, i * NK:(i + 1) * NK])
                if part == 1:
                    last.then_inc(searched, 1)

            def pairs(head):
                nc.vector.drain()
                nc.vector.tensor_tensor(pair, spread(best[:, 0], 3, TOP), spread(best[:, 1], 2, TOP), ALU.add)
                nc.vector.tensor_copy(best_at_f[:], best_at[:])
                nc.vector.drain()
                for t in range(NTF):
                    nc.vector.max(top[:, t, :], pair[:, t].rearrange("p x y -> p (x y)"))
                nc.vector.drain()
                for t in range(NTF):
                    nc.vector.max_index(at[:, t, :], top[:, t, :], pair[:, t].rearrange("p x y -> p (x y)"))
                nc.vector.tensor_tensor(soft[:], top[:], spread(top[:, :, 0], 2, TOP), ALU.subtract)\
                    .then_inc(soft_in, 1)

            def choice(head):
                nc.vector.drain()
                flat = at[:].rearrange("p t k -> p (t k)")
                nc.vector.tensor_scalar(at_xy[:, 0, :], flat, 3, None, ALU.logical_shift_right)
                nc.vector.tensor_scalar(at_xy[:, 1, :], flat, TOP - 1, None, ALU.bitwise_and)
                nc.vector.drain()
                nc.vector.tensor_copy(at_f[:], at_xy[:])
                for half in range(2):
                    nc.vector.drain()
                    nc.vector.tensor_tensor(match.rearrange("p t k j -> p (t k) j"), spread(at_f[:, half, :], 2, TOP),
                                            spread(eight[:], 1, PICK), ALU.is_equal)
                    nc.vector.drain()
                    nc.vector.tensor_tensor(match, match, spread(best_at_f[:, half], 2, TOP), ALU.mult)
                    nc.vector.drain()
                    nc.vector.tensor_reduce(chosen[:, half, :], match.rearrange("p t k j -> p (t k) j"), AX_X,
                                            ALU.add)
                nc.vector.drain()
                dve.wait_ge(soft_out, head + 1)
                nc.vector.tensor_reduce(soft_sum[:], soft[:], AX_X, ALU.add)
                nc.vector.scalar_tensor_tensor(idx_next[:], chosen[:, 0, :], float(NK), chosen[:, 1, :], ALU.mult,
                                               ALU.add).then_inc(idx_ready, 1)
                nc.vector.drain()
                nc.vector.reciprocal(soft_sum[:], soft_sum[:])
                nc.vector.drain()
                nc.vector.tensor_tensor(gate_next[:].rearrange("p (t k) -> p t k", k=TOP), soft[:],
                                        spread(soft_sum[:], 2, TOP), ALU.mult)

            def steps(head, k):
                for stage, half, part in DVE_STEPS.get(k, ()):
                    if stage == "affine":
                        affine(head, half)
                    elif stage == "search":
                        search(head, half, part)
                    elif stage == "pairs":
                        pairs(head)
                    else:
                        choice(head)

            def weights(h, t):
                s = t % 2
                dve.wait_ge(tanh_ready, NTF * h + t + 1)
                nc.vector.scalar_tensor_tensor(tanh[:, s, :], tanh[:, s, :], 1.0, hidden[:, s, :], ALU.add, ALU.mult)
                nc.vector.drain()
                nc.vector.scalar_tensor_tensor(weight[:, s, :], tanh[:, s, :], 0.5, gate[:, t * TOP:(t + 1) * TOP],
                                               ALU.mult, ALU.mult).then_inc(weight_ready, 1)

            def add_rows(h, t):
                dve.wait_ge(rows_used, 2 * (NTF * h + t) + 2 + RING)
                nc.vector.tensor_tensor(acc[:, t, :], acc[:, t, :], ps_out[t % 2][:], ALU.add).then_inc(acc_done, 1)

            def start(h):
                nc.vector.drain()
                nc.vector.tensor_copy(gate[:], gate_next[:])
                nc.vector.drain()

            def unit(h, t, step):
                s = t % 2
                for k in range(TOP):
                    v = 2 * t + k // HU
                    if k % HU == 0:
                        dve.wait_ge(rows_in[v % RING], 16 * HU * (uses(v % RING) * h + v // RING + 1))
                    down = rows[:, v % RING, k % HU, 0:D]
                    nc.vector.tensor_tensor_reduce(down, down, xn_all[:, t, :], 1.0, 0.0, ALU.mult, ALU.add,
                                                   hidden[:, s, k:k + 1])
                    if k == 1 and t >= 1:
                        weights(h, t - 1)
                    if k == HU and t >= 2:
                        add_rows(h, t - 2)
                nc.vector.drain()
                nc.vector.scalar_tensor_tensor(cubic[:, s, :], hidden[:, s, :], 0.044715, hidden[:, s, :],
                                               ALU.mult, ALU.mult)
                nc.vector.drain()
                nc.vector.scalar_tensor_tensor(cubic[:, s, :], cubic[:, s, :], 1.0, hidden[:, s, :], ALU.add,
                                               ALU.mult).then_inc(cubic_ready, 1)
                step()

            def finish(h):
                weights(h, NTF - 1)
                for t in (NTF - 2, NTF - 1):
                    add_rows(h, t)

            dve.sem_inc(acc_done, 2)
            dve.wait_ge(small_in, 32)
            dve.wait_ge(iota_ready, 1)
            run_heads(dve, steps, start, unit, finish)

        @block.scalar
        def _(act):
            def affine(head, half):
                n = nth(head, half)
                act.wait_ge(bn_var, n + 1)
                nc.scalar.activation(std[:], var_eps[:], ACT.Sqrt).then_inc(bn_std, 1)
                act.wait_ge(affine_ready, n + 1)
                if not (first(head) and half == 0):
                    act.wait_ge(searched, n)
                for c in range(QC):
                    nc.scalar.activation(q_t[:, c * QN:(c + 1) * QN], ps_q[c][:, 0:QN], ACT.Identity,
                                         bias=shift[:], scale=scale[:]).then_inc(q_ready, 1)

            def match_out(head, half, part):
                n = nth(head, half)
                for g in (2 * part, 2 * part + 1):
                    act.wait_ge(sims_made, NG * n + g + 1)
                    tiles = group(g)
                    nc.scalar.copy(q_t[:, tiles[0] * NK:(tiles[-1] + 1) * NK], ps_m[g % 2][:, 0:len(tiles) * NK])\
                        .then_inc(sims_ready, 1)

            def soften(head):
                act.wait_ge(soft_in, head + 1)
                nc.scalar.activation(soft[:], soft[:], ACT.Exp).then_inc(soft_out, 1)

            def steps(head, k):
                for stage, half, part in ACT_STEPS.get(k, ()):
                    if stage == "affine":
                        affine(head, half)
                    elif stage == "match":
                        match_out(head, half, part)
                    else:
                        soften(head)

            def diagonals(h, t):
                act.wait_ge(weight_ready, NTF * h + t + 1)
                for k in range(TOP):
                    if k % HU == 0:
                        act.wait_ge(rows_used, 2 * (NTF * h + t) + k // HU - 1 + RING)
                    nc.scalar.activation(diag[:, k, :], ident[:], ACT.Copy, scale=weight[:, t % 2, k:k + 1])\
                        .then_inc(diag_ready, 1)

            def unit(h, t, step):
                if t >= 1:
                    diagonals(h, t - 1)
                act.wait_ge(cubic_ready, NTF * h + t + 1)
                nc.scalar.activation(tanh[:, t % 2, :], cubic[:, t % 2, :], ACT.Tanh, scale=GELU_C)\
                    .then_inc(tanh_ready, 1)
                step()

            run_heads(act, steps, lambda h: None, unit, lambda h: diagonals(h, NTF - 1))


def build(nc, a, out):
    x2_dram = nc.dram_tensor("x2_dram", [TOK, D], F32, kind="Internal").ap()
    build_attention(nc, a, x2_dram)
    with ExitStack() as ctx:
        def sb(name, shape):
            return ctx.enter_context(nc.sbuf_tensor(name, shape, F32))

        acc = sb("acc", [P, NTF, D])
        xn_all = sb("xn_all", [P, NTF, D])
        xn_t = sb("xn_t", [P, KC, TOK])
        ident = sb("ident_f", [P, P])
        with ExitStack() as setup:
            ready = setup.enter_context(nc.semaphore("ident_ready"))
            block = setup.enter_context(nc.Block())

            @block.gpsimd
            def _(pool):
                nc.gpsimd.memset(ident[:], 0.0).then_inc(ready, 1)
                pool.wait_ge(ready, 1)
                nc.gpsimd.affine_select(out=ident[:], in_=ident[:], compare_op=ALU.not_equal, fill=1.0, base=0,
                                        pattern=[[-1, P]], channel_multiplier=1)

        build_norm(nc, x2_dram, acc, xn_all, xn_t, ident)
        build_experts(nc, a, out, acc, xn_all, xn_t, ident)


def kernel(**inputs):
    import numpy as np
    import concourse.bacc as bacc
    from concourse import mybir as mb
    from concourse.bass_utils import run_bass_kernel_spmd as run

    rows = np.concatenate([np.arange(h * HD, (h + 1) * HD) for h in HEADS])
    qkv = inputs["L0_attn_qkv_w"].reshape(3, D, D)[:, rows, :].reshape(3 * D, D)
    half = HD // 2
    freqs = np.outer(np.arange(S, dtype=np.float32),
                     1.0 / 10000.0 ** (np.arange(0, HD, 2, dtype=np.float32) / HD)).astype(np.float32)
    cos, sin = np.cos(freqs).astype(np.float32), np.sin(freqs).astype(np.float32)
    arrays = {
        "x": inputs["x"],
        "ctx_t": inputs["ctx_1024"].transpose(0, 2, 1),
        "mask": inputs["mask_1x1xSxS2_fk0"].reshape(S, SC),
        "w_qkv_t": qkv.T,
        "w_proj_t": inputs["L0_attn_proj_w"][:, rows].T,
        "proj_b": inputs["L0_attn_proj_b"],
        "curv": np.broadcast_to(inputs["L0_attn_curvature"].reshape(1, N_HYP), (P, N_HYP)),
        "rot_cos": np.concatenate([cos, cos], axis=1),
        "rot_sin": np.concatenate([sin, -sin], axis=1),
        "wq": inputs["L0_xattn_Wq"], "wk": inputs["L0_xattn_Wk"], "wv": inputs["L0_xattn_Wv"],
        "wo": inputs["L0_xattn_Wo"], "bq": inputs["L0_xattn_bq"].reshape(KC, P).T, "bk": inputs["L0_xattn_bk"].reshape(KC, P).T,
        "bv": inputs["L0_xattn_bv"], "bo": inputs["L0_xattn_bo"],
        "ffn_wq": inputs["L0_ffn_w_q"],
        "gamma": inputs["L0_ffn_bn_gamma"].reshape(NF, KD).T,
        "beta": inputs["L0_ffn_bn_beta"].reshape(NF, KD).T,
        "keys_t": inputs["L0_ffn_keys"].transpose(3, 2, 0, 1).reshape(KD, NF * NK),
        "experts": np.concatenate([inputs["L0_ffn_down_embed"], inputs["L0_ffn_up_embed"]], axis=1),
    }
    arrays = {k: np.ascontiguousarray(v) for k, v in arrays.items()}
    nc = bacc.Bacc("TRN2", target_bir_lowering=False, num_devices=1)
    aps = {k: nc.dram_tensor("in_" + k, v.shape, mb.dt.from_np(v.dtype), kind="ExternalInput").ap() for k, v in arrays.items()}
    out = nc.dram_tensor("out_0", (B, S, D), mb.dt.float32, kind="ExternalOutput").ap()
    build(nc, aps, out)
    return run(nc, [{"in_" + k: v for k, v in arrays.items()}], core_ids=[0]).results[0]["out_0"]
```
